# Optimizing a Trainium2 kernel written in Bass

```python
import numpy as np
import jax
import jax.numpy as jnp

def _softmax(x, axis=-1):
    return jax.nn.softmax(x, axis=axis)

def _gelu(x):
    return jax.nn.gelu(x, approximate=True)

def _silu(x):
    return jax.nn.silu(x)

def _sigmoid(x):
    return jax.nn.sigmoid(x)

def _layernorm(x, axis=-1, eps=1e-05):
    m = jnp.mean(x, axis=axis, keepdims=True)
    v = jnp.var(x, axis=axis, keepdims=True)
    return (x - m) / jnp.sqrt(v + eps)

def _scatter_add(tgt, idx, src, axis=0):
    return tgt.at[idx].add(src)

def _segment_sum(src, seg, n):
    return jax.ops.segment_sum(src, seg, n)
kernel_name = 'mk_early_fusion_d1_tok_img256_r4_0d6dc0'

def setup_inputs(seed: int=0):
    np.random.seed(seed)
    _w = jnp.asarray

    def _rec_inputs():
        import jax
        import jax.numpy as jnp
        _rk = jax.random.key(seed)
        x = -7.10856e-05 + 0.999911 * jax.random.normal(jax.random.fold_in(_rk, 1), (2, 64, 128, 64), jnp.float32)
        txt = -0.000161634 + 0.479995 * jax.random.normal(jax.random.fold_in(_rk, 2), (2, 128, 64), jnp.float32)
        return (x, txt)
    x, txt = _rec_inputs()

    def _L0_tok_setup():
        import jax, jax.numpy as jnp
        import numpy as np
        PATCH_LEN = 16
        STRIDE = 8
        PAD = 8
        key = jax.random.key(seed)
        k1, k2 = jax.random.split(key)
        x = jax.random.normal(k1, (32, 64, 128, 64), dtype=jnp.float32)
        in_feat = 64 * (PATCH_LEN // 2 + 1) * 2
        W = jax.random.normal(k2, (64, in_feat), dtype=jnp.float32) * 0.02
        return {'x': x, 'W': W}
    _L0_tok_all = _L0_tok_setup()
    _L0_tok_in = {k: v for k, v in _L0_tok_all.items() if k in ('W',)}
    del _L0_tok_all

    def _L0_attn_setup():
        import math
        import jax, jax.numpy as jnp
        import numpy as np
        EPS_DIV = 1e-07
        EPS_NORM = 1e-12

        def _l2_normalize(x, axis):
            n = jnp.sqrt(jnp.sum(x * x, axis=axis, keepdims=True))
            return x / jnp.maximum(n, EPS_NORM)
        key = jax.random.key(seed)
        ks = jax.random.split(key, 5)
        b, N, C = (8, 1024, 64)
        x = jax.random.normal(ks[0], (b, N, C), dtype=jnp.float32)
        W_qkv = jax.random.normal(ks[1], (C, 3 * C), dtype=jnp.float32) * (1.0 / math.sqrt(C))
        b_qkv = jax.random.normal(ks[2], (3 * C,), dtype=jnp.float32) * 0.02
        W_out = jax.random.normal(ks[3], (C, C), dtype=jnp.float32) * (1.0 / math.sqrt(C))
        b_out = jax.random.normal(ks[4], (C,), dtype=jnp.float32) * 0.02
        return {'x': x, 'W_qkv': W_qkv, 'b_qkv': b_qkv, 'W_out': W_out, 'b_out': b_out}
    _L0_attn_all = _L0_attn_setup()
    _L0_attn_in = {k: v for k, v in _L0_attn_all.items() if k in ('W_qkv', 'b_qkv', 'W_out', 'b_out')}
    del _L0_attn_all

    def _L0_ffn_setup():
        import jax, jax.numpy as jnp
        import numpy as np
        B, T, C = (64, 96, 64)
        NH, NKV = (4, 2)
        HD = C // NH
        NREP = NH // NKV
        NE, TOPK = (8, 2)
        HID = int(8 / 3 * C)
        EPS_RMS = 1e-06

        def _rope_tables(t_len):
            inv_freq = 1.0 / 10000.0 ** (np.arange(0, HD, 2, dtype=np.float32) / HD)
            t = np.arange(t_len, dtype=np.float32)
            freqs = np.outer(t, inv_freq)
            emb = np.concatenate([freqs, freqs], axis=-1)
            return (jnp.asarray(np.cos(emb)), jnp.asarray(np.sin(emb)))

        def _rotate_half(x):
            h = x.shape[-1] // 2
            return jnp.concatenate([-x[..., h:], x[..., :h]], axis=-1)

        def _rmsnorm(v, w):
            return v * jax.lax.rsqrt(jnp.mean(v * v, axis=-1, keepdims=True) + EPS_RMS) * w
        key = jax.random.key(seed)
        ks = jax.random.split(key, 10)
        s = lambda k, shape: jax.random.normal(k, shape, jnp.float32) * 0.02
        return {'x': jax.random.normal(ks[0], (B, T, C), jnp.float32), 'ln1_w': jnp.ones((C,), jnp.float32), 'ln2_w': jnp.ones((C,), jnp.float32), 'wq': s(ks[1], (NH * HD, C)), 'wk': s(ks[2], (NKV * HD, C)), 'wv': s(ks[3], (NKV * HD, C)), 'wo': s(ks[4], (C, C)), 'router_w': s(ks[5], (NE, C)), 'w1': s(ks[6], (NE, HID, C)), 'w2': s(ks[7], (NE, C, HID)), 'w3': s(ks[8], (NE, HID, C))}
    _L0_ffn_all = _L0_ffn_setup()
    _L0_ffn_in = {k: v for k, v in _L0_ffn_all.items() if k in ('ln1_w', 'ln2_w', 'wq', 'wk', 'wv', 'wo', 'router_w', 'w1', 'w2', 'w3')}
    del _L0_ffn_all
    return {'x': x, 'txt': txt, 'L0_tok_W': _L0_tok_in['W'], 'L0_attn_W_qkv': _L0_attn_in['W_qkv'], 'L0_attn_b_qkv': _L0_attn_in['b_qkv'], 'L0_attn_W_out': _L0_attn_in['W_out'], 'L0_attn_b_out': _L0_attn_in['b_out'], 'L0_ffn_ln1_w': _L0_ffn_in['ln1_w'], 'L0_ffn_ln2_w': _L0_ffn_in['ln2_w'], 'L0_ffn_wq': _L0_ffn_in['wq'], 'L0_ffn_wk': _L0_ffn_in['wk'], 'L0_ffn_wv': _L0_ffn_in['wv'], 'L0_ffn_wo': _L0_ffn_in['wo'], 'L0_ffn_router_w': _L0_ffn_in['router_w'], 'L0_ffn_w1': _L0_ffn_in['w1'], 'L0_ffn_w2': _L0_ffn_in['w2'], 'L0_ffn_w3': _L0_ffn_in['w3']}

def reference(x, txt, L0_tok_W, L0_attn_W_qkv, L0_attn_b_qkv, L0_attn_W_out, L0_attn_b_out, L0_ffn_ln1_w, L0_ffn_ln2_w, L0_ffn_wq, L0_ffn_wk, L0_ffn_wv, L0_ffn_wo, L0_ffn_router_w, L0_ffn_w1, L0_ffn_w2, L0_ffn_w3):
    import jax
    import jax.numpy as jnp

    def _L0_tok_ref(x, W):
        import jax, jax.numpy as jnp
        import numpy as np
        PATCH_LEN = 16
        STRIDE = 8
        PAD = 8
        B, C, T, V = x.shape
        xp = jnp.pad(x, ((0, 0), (0, 0), (0, PAD), (0, 0)), mode='edge')
        Tp = T + PAD
        N = (Tp - PATCH_LEN) // STRIDE + 1
        idx = jnp.arange(N)[:, None] * STRIDE + jnp.arange(PATCH_LEN)[None, :]
        patches = xp[:, :, idx, :]
        patches = jnp.transpose(patches, (0, 4, 2, 3, 1))
        xf = jnp.fft.rfft(patches, axis=-2, norm='ortho')
        F = xf.shape[-2]
        x_real = xf.real.reshape(B, V, N, F * C)
        x_imag = xf.imag.reshape(B, V, N, F * C)
        x_emb = jnp.concatenate([x_real, x_imag], axis=-1)
        x_emb = x_emb @ W.T
        return x_emb.reshape(B, V * N, -1)

    def _L0_attn_ref(x, W_qkv, b_qkv, W_out, b_out):
        import math
        import jax, jax.numpy as jnp
        import numpy as np
        EPS_DIV = 1e-07
        EPS_NORM = 1e-12

        def _l2_normalize(x, axis):
            n = jnp.sqrt(jnp.sum(x * x, axis=axis, keepdims=True))
            return x / jnp.maximum(n, EPS_NORM)
        b, N, C = x.shape
        qkv = x @ W_qkv + b_qkv
        q, k, v = jnp.split(qkv, 3, axis=2)
        q = q - jnp.mean(q, axis=2, keepdims=True)
        k = k - jnp.mean(k, axis=2, keepdims=True)
        q2 = q * q
        k2 = k * k
        q2s = jnp.sum(q2, axis=2, keepdims=True)
        k2s = jnp.sum(k2, axis=2, keepdims=True)
        k2 = _l2_normalize(k2 / (k2s + EPS_DIV), axis=-2)
        q2 = _l2_normalize(q2 / (q2s + EPS_DIV), axis=-1)
        kv = jnp.einsum('bnc,bnd->bcd', k2, v)
        t2 = jnp.einsum('bnc,bcd->bnd', q2, kv) / math.sqrt(N)
        attn = v + t2
        return attn @ W_out + b_out

    def _L0_ffn_ref(x, ln1_w, ln2_w, wq, wk, wv, wo, router_w, w1, w2, w3):
        import jax, jax.numpy as jnp
        import numpy as np
        B, T, C = (64, 96, 64)
        NH, NKV = (4, 2)
        HD = C // NH
        NREP = NH // NKV
        NE, TOPK = (8, 2)
        HID = int(8 / 3 * C)
        EPS_RMS = 1e-06

        def _rope_tables(t_len):
            inv_freq = 1.0 / 10000.0 ** (np.arange(0, HD, 2, dtype=np.float32) / HD)
            t = np.arange(t_len, dtype=np.float32)
            freqs = np.outer(t, inv_freq)
            emb = np.concatenate([freqs, freqs], axis=-1)
            return (jnp.asarray(np.cos(emb)), jnp.asarray(np.sin(emb)))

        def _rotate_half(x):
            h = x.shape[-1] // 2
            return jnp.concatenate([-x[..., h:], x[..., :h]], axis=-1)

        def _rmsnorm(v, w):
            return v * jax.lax.rsqrt(jnp.mean(v * v, axis=-1, keepdims=True) + EPS_RMS) * w
        Bx, Tx, Cx = x.shape
        h = _rmsnorm(x, ln1_w)
        q = (h @ wq.T).reshape(Bx, Tx, NH, HD).transpose(0, 2, 1, 3)
        k = (h @ wk.T).reshape(Bx, Tx, NKV, HD).transpose(0, 2, 1, 3)
        v = (h @ wv.T).reshape(Bx, Tx, NKV, HD).transpose(0, 2, 1, 3)
        cos, sin = _rope_tables(Tx)
        cos, sin = (cos[None, None], sin[None, None])
        q = q * cos + _rotate_half(q) * sin
        k = k * cos + _rotate_half(k) * sin
        k = jnp.repeat(k, NREP, axis=1)
        v = jnp.repeat(v, NREP, axis=1)
        scores = jnp.einsum('bhtd,bhsd->bhts', q, k) / jnp.sqrt(jnp.float32(HD))
        causal = jnp.tril(jnp.ones((Tx, Tx), dtype=bool))
        scores = jnp.where(causal[None, None], scores, jnp.float32(-1e+30))
        att = jax.nn.softmax(scores, axis=-1)
        y = jnp.einsum('bhts,bhsd->bhtd', att, v).transpose(0, 2, 1, 3).reshape(Bx, Tx, Cx)
        x = x + y @ wo.T
        flat = _rmsnorm(x, ln2_w).reshape(-1, Cx)
        probs = jax.nn.softmax(flat @ router_w.T, axis=-1)
        tp, ti = jax.lax.top_k(probs, TOPK)
        tp = tp / (jnp.sum(tp, axis=-1, keepdims=True) + 1e-09)
        weights = jnp.sum(tp[..., None] * jax.nn.one_hot(ti, NE, dtype=flat.dtype), axis=1)
        out = jnp.zeros_like(flat)
        for e in range(NE):
            hh = jax.nn.silu(flat @ w1[e].T) * (flat @ w3[e].T)
            out = out + weights[:, e:e + 1] * (hh @ w2[e].T)
        return x + out.reshape(Bx, Tx, Cx)
    h = _L0_tok_ref(x, L0_tok_W)
    h = jnp.concatenate([h, txt], axis=1)
    h = h + _L0_attn_ref(_layernorm(h, axis=-1), L0_attn_W_qkv, L0_attn_b_qkv, L0_attn_W_out, L0_attn_b_out)
    h = h + _L0_ffn_ref(_layernorm(h, axis=-1), L0_ffn_ln1_w, L0_ffn_ln2_w, L0_ffn_wq, L0_ffn_wk, L0_ffn_wv, L0_ffn_wo, L0_ffn_router_w, L0_ffn_w1, L0_ffn_w2, L0_ffn_w3)
    return h

_drawn_inputs = setup_inputs


def setup_inputs(seed=0):
    import zlib

    import numpy as np

    out = dict(_drawn_inputs(seed))
    spreads = {'L0_ffn_ln1_w': (1.0, 0.6), 'L0_ffn_ln2_w': (1.0, 0.6)}
    factors = {'L0_attn_b_out': 3.265,
     'L0_ffn_wq': 8.0,
     'L0_ffn_wk': 8.0,
     'L0_ffn_wv': 8.0,
     'L0_ffn_wo': 8.0,
     'L0_ffn_router_w': 8.0,
     'L0_ffn_w1': 8.0,
     'L0_ffn_w2': 8.0,
     'L0_ffn_w3': 8.0}
    for name, (base, spread) in spreads.items():
        noise = np.random.default_rng([zlib.crc32(name.encode()), seed]).standard_normal(out[name].shape)
        drawn = base * np.exp(spread * noise) if base else spread * noise
        out[name] = jnp.asarray(drawn.astype(out[name].dtype))
    for name, factor in factors.items():
        out[name] = (out[name] * factor).astype(out[name].dtype)
    return out
```

```python
from contextlib import ExitStack

import concourse.bass as bass
from concourse import mybir

F32 = mybir.dt.float32
F32R = mybir.dt.float32r
BF16 = mybir.dt.bfloat16
U32 = mybir.dt.uint32
ALU = mybir.AluOpType
ACT = mybir.ActivationFunctionType
AX = mybir.AxisListType

P = 128
B, C, T, V = 2, 64, 128, 64
PATCH, STRIDE = 16, 8
NBLK = T // STRIDE + 1
NPATCH = T // STRIDE
NF = 2 * (PATCH // 2 + 1)
RUN = 4
TOK = V * NPATCH
TXT = 128
L = TOK + TXT
TILES = L // P
GT = 3
GROUPS = TILES // GT
NG = B * GROUPS
NT = B * TILES
GW = GT * P
NH, NKV, HD = 4, 2, 16
NE, HID = 8, 170
NCH = NE * HID
PAIRS = NE // 2
CUT = (0, 114, 226, 340)
CHUNKS = PAIRS * 3
HIDP = 114
SCORE_ROWS = 66
WCOLS = 2 * NCH + NE
LN_SCALE = 2.0 ** 40
LN2_20 = 20 * 0.6931471805599453
NEG = -1e30
PRING = 4


def chunk(c):
    return (c // 3) * 2 * HID + CUT[c % 3], CUT[c % 3 + 1] - CUT[c % 3]


def s1_units(tile):
    n = (tile % TILES + 1) * P
    return [(h, k, min(512, n - k), k + 512 >= n) for k in range(0, n, 512) for h in range(NH)]


def s1_chunks(tile):
    return -(-(tile % TILES + 1) * P // 512)


S1_DURING = [[3, 4, 5], [6, 7, 8], [9, 10, 11, 12, 13], [14, 15], [16, 17], []]


def attention_steps():
    plan = []
    for n in range(NG):
        steps = GT * (n % GROUPS) + GT
        todo = list(S1_DURING[n])
        every = max(1, steps // max(1, len(todo)))
        pending = None
        for j in range(steps):
            new = todo.pop(0) if todo and j % every == 0 else None
            plan.append((n, j, pending if new is not None else None, new))
            pending = new if new is not None else pending
        assert not todo
        plan.append((n, None, pending, None))
    return plan


def build(nc, x, txt, w_tok, w_qkv, b_qkv, w_vT, w_out, b_out, ln1, ln2, w_ffn, woT, routerT, w1T, w3T, w2T, dft, consts, out):
    with ExitStack() as ctx:
        def sb(name, shape, dt=F32):
            return ctx.enter_context(nc.sbuf_tensor(name, shape, dt))

        def sem(name):
            return ctx.enter_context(nc.semaphore(name))

        X = sb("X", [P, B, NBLK, RUN, V])
        early = sb("early", [P, 2 * NG * GW])
        Wt = early[0:NF, 0:C * C].rearrange("p (o c) -> p o c", c=C)
        xnT = early[0:C + 1, 0:NG * GW].rearrange("p (n q) -> p n q", n=NG)
        q2T = early[0:C, NG * GW:2 * NG * GW].rearrange("p (n q) -> p n q", n=NG)
        work = sb("work", [P, 16 * GT * C])
        WR = work[:, 0:WCOLS]
        cut = lambda first, k, pat, **kw: work[:, first * GT * C:(first + 2 * k) * GT * C].rearrange(pat, s=2, c=C, **kw)
        SQ = cut(0, 1, "p (s t c) -> p s t c", t=GT)
        QK2 = cut(2, 2, "p (s t a c) -> p s t a c", t=GT, a=2)
        Q4 = cut(6, 1, "p (s t c) -> p s t c", t=GT)
        KK = cut(8, 2, "p (s t a c) -> p s t a c", t=GT, a=2)
        Q2 = cut(12, 1, "p (s t c) -> p s t c", t=GT)
        HN = cut(14, 1, "p (s t c) -> p s t c", t=GT)
        WH = sb("WH", [P, WCOLS], F32R)
        WL = sb("WL", [P, WCOLS], F32R)
        W2 = sb("W2", [HIDP, CHUNKS, P])
        G = sb("G", [P, 2, RUN, 64])
        dft_sb = sb("dft_sb", [NF, PATCH])
        cst = sb("cst", [P, 128 + 2 * TILES * HD + NE])
        ident = cst[:, 0:128]
        cos = cst[:, 128:128 + TILES * HD].rearrange("p (t e) -> p t e", e=HD)
        sin = cst[:, 128 + TILES * HD:128 + 2 * TILES * HD].rearrange("p (t e) -> p t e", e=HD)
        iota = cst[:, 128 + 2 * TILES * HD:128 + 2 * TILES * HD + NE]
        identb = sb("identb", [P, P], BF16)
        maskb = sb("maskb", [P, P], BF16)
        bias = sb("bias", [P, 4])
        b_eps5, b_eps6, b_zero, b_20 = (bias[:, i:i + 1] for i in range(4))
        ln1_sb = sb("ln1_sb", [C, 1])
        ln2_sb = sb("ln2_sb", [P, 1])
        Wqkv = sb("Wqkv", [C + 1, 192])
        wmean = sb("wmean", [C + 1, 2])
        WvT = sb("WvT", [C, C + 1])
        Wout = sb("Wout", [C, C])
        bout = sb("bout", [C + 1, C])
        WVO = sb("WVO", [C + 1, C])
        KVS = sb("KVS", [C, B, C])
        KVST = sb("KVST", [C, B, C])
        KVO = sb("KVO", [C, B, C])
        Wffn = sb("Wffn", [C, P])
        WoT = sb("WoT", [C, C])
        st = sb("st", [P, NG, 64])
        kst = sb("kst", [C, B, 4])
        H = sb("H", [P, NT, C])
        D = sb("D", [P, NT, C])
        V1 = sb("V1", [P, 2, GT, C + 1])
        feat = sb("feat", [P, 2, GW])
        hfm = feat[:, :, :].rearrange("p s q -> p (s q)")[:, 0:TOK // 2]
        hnT = feat[0:C, :, :]
        yT = feat[0:C, :, :]
        QKs = sb("QKs", [P, 2, GT, 6, HD])
        RT = sb("RT", [P, 2, 2, GT, 6, HD])
        HL = sb("HL", [P, 2, GT, 6, 4, HD], F32R)
        QT = sb("QT", [SCORE_ROWS, NH, NT * P], F32R)
        KT = sb("KT", [SCORE_ROWS, NKV, NT * P], F32R)
        VA = sb("VA", [P, NT, NKV, 32])
        MXC = sb("MXC", [P, NT, NH, 3])
        NM = sb("NM", [P, NT, NH])
        ML = sb("ML", [P, NT, NH, 2], F32R)
        Xf = X[:, :, :, :, :].rearrange("p b k r v -> p (b k r v)")
        PR = Xf[:, 0:PRING * NH * GW].rearrange("p (s h q) -> p s h q", s=PRING, h=NH)
        yo = PRING * NH * GW
        YS = Xf[:, yo:yo + 2 * GW].rearrange("p (s q) -> p s q", s=2)
        YN = Xf[:, yo + 2 * GW:yo + 2 * GW + NT * C].rearrange("p (t h e) -> p t h e", h=NH, e=HD)
        FL = sb("FL", [P, 2, GT, 2, C], F32R)
        FT = sb("FT", [P, NG, GW], F32R)
        RL = sb("RL", [P, NT, NE])
        TOP = sb("TOP", [P, NT, NE])
        IDX = sb("IDX", [P, NT, NE], U32)
        IDF = sb("IDF", [P, NT, 2])
        WA = sb("WA", [P, NT, NE])
        WB = sb("WB", [P, NT, NE])
        SI = Xf[0:HIDP, 0:3 * GW].rearrange("p (s q) -> p s q", s=3)
        HH = Xf[0:HIDP, 3 * GW:6 * GW].rearrange("p (s q) -> p s q", s=3)
        YW = Xf[:, 6 * GW:6 * GW + 3 * NE * C].rearrange("p (s e c) -> p s e c", s=3, e=NE)

        bank = [ctx.enter_context(nc.psum_tensor(f"bank{i}", [P, 512], F32)) for i in range(2)]
        wide = [ctx.enter_context(nc.psum_tensor(f"wide{i}", [P, 2, 512], F32)) for i in range(2)]
        bank += [wide[0][:, 0, :], wide[0][:, 1, :], wide[1][:, 0, :], wide[1][:, 1, :]]
        bank += [ctx.enter_context(nc.psum_tensor(f"bank{i}", [P, 512], F32)) for i in (6, 7)]

        names = """s_x0 s_x1 s_wtok s_cst s_wa s_wf s_w2 s_txt s_out
            g_ready g_done c_bf c_bias c_ones w_split w_small w2_zero wvo_ready wvo_done bout_zero
            tok_done h_fm h_tp h_copied a_mean a_sq a_var a_rstd a_xn a_tp a_xT a_qkv a_sqr a_r a_q4 a_kk a_n2 a_rq a_f a_q2n
            a_kv a_q2tp a_q2T p_c p_rc p_kvs p_tp p_kvT p_kvo p_kvoS
            b_o b_h1 b_mean b_sq b_var b_rstd b_ms b_r1 b_hn b_h2 b_tp b_hT b_q b_qk b_hl b_qt b_qT b_kT
            s_done s_max s_nm s_ml s_mt s_mT st_done e_done m_done pv_done y_cp y_tp y_n misc_free
            w_tp w_yT w_o w_x2 w_sq w_ss w_rs w_fl w_ft w_fT w_r w_lg w_e w_wt
            m_a m_b m_s m_h m_y m_yw m_tr
            ve_chain ac_chain po_chain""".split()
        z = {n: sem(n) for n in names}

        block = ctx.enter_context(nc.Block())

        def wave(stages):
            for s in range(NG + len(stages) - 1):
                for k in reversed(range(len(stages))):
                    if 0 <= s - k < NG:
                        stages[k](s - k)

        def linker(eng, chain):
            count = [0]

            def link(ins):
                count[0] += 1
                ins.then_inc(chain, 1)
                eng.wait_ge(chain, count[0])
            return link

        def bc(ap, shape):
            return ap.unsqueeze(len(ap.shape)).to_broadcast(shape)

        def tiles(n):
            return slice(GT * n, GT * n + GT)

        @block.sync
        def _(sp):
            sp.dma_start(dft_sb[:, :], dft).then_inc(z["s_wtok"], 16)
            sp.dma_start(Wt[:, :, :], w_tok).then_inc(z["s_wtok"], 16)
            for b in range(B):
                xb = x[b].rearrange("c (k h r) v -> h c k r v", h=2, r=RUN)
                for h in range(2):
                    sp.dma_start(X[64 * h:64 * h + 64, b, 0:NBLK - 1, :, :], xb[h]).then_inc((z["s_x0"], z["s_x1"])[b], 16)
                last = x[b][:, T - 1:T, :]
                for h in range(2):
                    for r in range(RUN):
                        sp.dma_start(X[64 * h:64 * h + 64, b, NBLK - 1, r:r + 1, :], last).then_inc((z["s_x0"], z["s_x1"])[b], 16)
            for n in range(NG):
                b, g = divmod(n, GROUPS)
                sp.wait_ge(z["m_tr"], GT * n + GT)
                sp.dma_start(out[b, GW * g:GW * g + GW, :].rearrange("(t p) c -> p t c", p=P), H[:, tiles(n), :]).then_inc(z["s_out"], 16)
            sp.wait_ge(z["s_out"], 16 * NG)

        @block.gpsimd
        def _(po):
            link = linker(po, z["po_chain"])
            po.memset(bias[:, 0:1], 1e-5)
            po.memset(bias[:, 1:2], 1e-6)
            po.memset(bias[:, 2:3], 0.0)
            po.memset(bias[:, 3:4], LN2_20).then_inc(z["c_bias"], 1)
            link(po.memset(identb[:, :], 0.0))
            link(po.memset(maskb[:, :], 0.0))
            po.affine_select(out=identb[:, :], in_=identb[:, :], compare_op=ALU.not_equal, fill=1.0, base=0,
                             pattern=[[-1, P]], channel_multiplier=1).then_inc(z["c_bf"], 1)
            po.affine_select(out=maskb[:, :], in_=maskb[:, :], compare_op=ALU.is_ge, fill=NEG, base=0,
                             pattern=[[-1, P]], channel_multiplier=1).then_inc(z["c_bf"], 1)
            po.memset(W2[:, :, :], 0.0).then_inc(z["w2_zero"], 1)
            po.memset(bout[:, :], 0.0).then_inc(z["bout_zero"], 1)
            link(po.memset(VA[:, :, :, :], 0.0))
            po.memset(VA[:, :, :, HD:HD + 1], 1.0)
            po.memset(V1[:, :, :, C:C + 1], 1.0).then_inc(z["c_ones"], 1)

            po.wait_ge(z["s_wf"], 16 * 8)
            link(po.tensor_scalar(WR[:, :], WR[:, :], ln2_sb[:, 0:1], None, ALU.mult))
            link(po.tensor_copy(WH[:, :], WR[:, :]))
            po.tensor_tensor(WL[:, :], WR[:, :], WH[:, :], ALU.subtract).then_inc(z["w_split"], 1)
            po.wait_ge(z["w_split"], 1)

            def center(n, mean, src, mean_sem, sq_sem):
                po.wait_ge(mean_sem, n + 1)
                link(po.tensor_tensor(D[:, tiles(n), :], src, bc(mean, [P, GT, C]), ALU.add))
                po.tensor_tensor(SQ[:, n % 2, :, :], D[:, tiles(n), :], D[:, tiles(n), :], ALU.mult).then_inc(sq_sem, 1)

            def a_center(n):
                center(n, st[:, n, 3:6], H[:, tiles(n), :], z["a_mean"], z["a_sq"])
                po.wait_ge(z["a_rstd"], n + 1)
                po.tensor_tensor(D[:, tiles(n), :], D[:, tiles(n), :], bc(st[:, n, 12:15], [P, GT, C]), ALU.mult).then_inc(z["a_xn"], 1)

            def a_norms(n):
                r = st[:, n, 21:27].rearrange("p (t two) -> p t two", two=2)
                q, k = QK2[:, n % 2, :, 0, :], QK2[:, n % 2, :, 1, :]
                po.wait_ge(z["a_sqr"], 2 * n + 2)
                po.tensor_tensor(Q4[:, n % 2, :, :], q, q, ALU.mult).then_inc(z["a_q4"], 1)
                po.wait_ge(z["a_r"], n + 1)
                if n >= 2:
                    po.wait_ge(z["a_kv"], n - 1)
                link(po.tensor_tensor(KK[:, n % 2, :, 0, :], k, bc(r[:, :, 1], [P, GT, C]), ALU.mult))
                po.tensor_tensor(KK[:, n % 2, :, 1, :], KK[:, n % 2, :, 0, :], KK[:, n % 2, :, 0, :], ALU.mult).then_inc(z["a_kk"], 1)
                po.wait_ge(z["a_f"], n + 1)
                if n >= 2:
                    po.wait_ge(z["a_q2tp"], n - 1)
                po.tensor_tensor(Q2[:, n % 2, :, :], q, bc(st[:, n, 36:39], [P, GT, C]), ALU.mult).then_inc(z["a_q2n"], 1)

            wave([lambda n: None, a_center, lambda n: None, a_norms, lambda n: None])

            def b_center(n):
                center(n, st[:, n, 3:6], H[:, tiles(n), :], z["b_mean"], z["b_sq"])
                po.wait_ge(z["b_r1"], n + 1)
                if n >= 2:
                    po.wait_ge(z["b_tp"], n - 1)
                link(po.tensor_tensor(st[:, n, 21:24], st[:, n, 12:15], st[:, n, 18:21], ALU.mult))
                po.tensor_tensor(HN[:, n % 2, :, :], D[:, tiles(n), :], bc(st[:, n, 21:24], [P, GT, C]), ALU.mult).then_inc(z["b_hn"], 1)
                po.tensor_tensor(D[:, tiles(n), :], D[:, tiles(n), :], bc(st[:, n, 12:15], [P, GT, C]), ALU.mult).then_inc(z["b_h2"], 1)

            def b_rope(n):
                g = n % GROUPS
                s = n % 2
                shape = [P, GT, 6, HD // 2]
                cb = cos[:, GT * g:GT * g + GT, :].unsqueeze(2).to_broadcast([P, GT, 6, HD])
                sn = sin[:, GT * g:GT * g + GT, :].unsqueeze(2)
                po.wait_ge(z["b_qk"], 2 * n + 2)
                po.tensor_tensor(RT[:, s, 0], QKs[:, s], cb, ALU.mult)
                po.tensor_tensor(RT[:, s, 1, :, :, 0:8], QKs[:, s, :, :, 8:16], sn[:, :, :, 0:8].to_broadcast(shape), ALU.mult)
                link(po.tensor_tensor(RT[:, s, 1, :, :, 8:16], QKs[:, s, :, :, 0:8], sn[:, :, :, 8:16].to_broadcast(shape), ALU.mult))
                link(po.tensor_tensor(RT[:, s, 0], RT[:, s, 0], RT[:, s, 1], ALU.add))
                if n >= 2:
                    po.wait_ge(z["b_qt"], GT * (n - 1))
                link(po.tensor_copy(HL[:, s, :, :, 0, :], RT[:, s, 0]))
                link(po.tensor_tensor(HL[:, s, :, :, 1, :], RT[:, s, 0], HL[:, s, :, :, 0, :], ALU.subtract))
                for slot in range(2):
                    po.tensor_copy(HL[:, s, :, 0:NH, 2 + slot, :], HL[:, s, :, 0:NH, 1 - slot, :])
                po.tensor_copy(HL[:, s, :, NH:6, 2:4, :].rearrange("p t h a e -> p t h (a e)"),
                               HL[:, s, :, NH:6, 0:2, :].rearrange("p t h a e -> p t h (a e)")).then_inc(z["b_hl"], 1)

            wave([b_center, lambda n: None, b_rope, lambda n: None])
            def m_split(t):
                po.wait_ge(z["s_nm"], t + 1)
                link(po.tensor_copy(ML[:, t, :, 0], NM[:, t, :]))
                po.tensor_tensor(ML[:, t, :, 1], NM[:, t, :], ML[:, t, :, 0], ALU.subtract).then_inc(z["s_ml"], 1)

            for t in range(GT):
                m_split(t)
            jj = 0
            for n, j, finished, _ in attention_steps():
                if finished is not None:
                    m_split(finished)
                if j is None:
                    continue
                jj += 1
                if j >= GT * (n % GROUPS):
                    q0 = P * (j - GT * (n % GROUPS))
                    po.wait_ge(z["e_done"], 2 * jj)
                    dia = PR[:, (jj - 1) % PRING, :, q0:q0 + P]
                    po.affine_select(out=dia, in_=dia, compare_op=ALU.is_ge, fill=0.0, base=0,
                                     pattern=[[0, NH], [1, P]], channel_multiplier=-1).then_inc(z["m_done"], 1)

            def w_norm(n):
                po.wait_ge(z["w_x2"], n + 1)
                po.tensor_tensor(SQ[:, n % 2, :, :], D[:, tiles(n), :], D[:, tiles(n), :], ALU.mult).then_inc(z["w_sq"], 1)
                po.tensor_tensor(H[:, tiles(n), :], H[:, tiles(n), :], D[:, tiles(n), :], ALU.add)
                po.wait_ge(z["w_rs"], n + 1)
                link(po.tensor_tensor(D[:, tiles(n), :], D[:, tiles(n), :], bc(st[:, n, 33:36], [P, GT, C]), ALU.mult))
                if n >= 2:
                    po.wait_ge(z["w_ft"], n - 1)
                link(po.tensor_copy(FL[:, n % 2, :, 0, :], D[:, tiles(n), :]))
                po.tensor_tensor(FL[:, n % 2, :, 1, :], D[:, tiles(n), :], FL[:, n % 2, :, 0, :], ALU.subtract).then_inc(z["w_fl"], 1)

            wave([lambda n: None, w_norm, lambda n: None, lambda n: None])

            for n in range(NG):
                for r in range(GT):
                    t = GT * n + r
                    y = YW[:, t % 3]
                    po.wait_ge(z["m_yw"], t + 1)
                    link(po.tensor_tensor(y[:, 0:4, :], y[:, 0:4, :], y[:, 4:8, :], ALU.add))
                    link(po.tensor_tensor(y[:, 0:2, :], y[:, 0:2, :], y[:, 2:4, :], ALU.add))
                    link(po.tensor_tensor(y[:, 0, :], y[:, 0, :], y[:, 1, :], ALU.add))
                    ins = po.tensor_tensor(H[:, t, :], H[:, t, :], y[:, 0, :], ALU.add)
                    ins.then_inc(z["m_tr"], 1)

        @block.scalar
        def _(ac):
            link = linker(ac, z["ac_chain"])
            ac.dma_start(cst[:, :], consts).then_inc(z["s_cst"], 16)
            ac.dma_start(Wqkv[0:C, :], w_qkv).then_inc(z["s_wa"], 16)
            ac.dma_start(Wqkv[C:C + 1, :], b_qkv).then_inc(z["s_wa"], 16)
            ac.dma_start(WvT[:, :], w_vT).then_inc(z["s_wa"], 16)
            ac.dma_start(Wout[:, :], w_out).then_inc(z["s_wa"], 16)
            ac.dma_start(Wffn[:, :], w_ffn).then_inc(z["s_wa"], 16)
            ac.dma_start(WoT[:, :], woT).then_inc(z["s_wa"], 16)
            ac.dma_start(ln1_sb[:, :], ln1).then_inc(z["s_wa"], 16)
            ac.wait_ge(z["bout_zero"], 1)
            ac.dma_start(bout[C:C + 1, :], b_out).then_inc(z["s_wa"], 16)
            for b in range(B):
                ac.dma_start(H[:, TILES * (b + 1) - 1, :], txt[b]).then_inc(z["s_txt"], 16)
            for h in range(2):
                rows = slice(64 * h, 64 * h + 64)
                ac.dma_start(ln2_sb[rows, :], ln2).then_inc(z["s_wf"], 16)
                ac.dma_start(WR[rows, 0:NCH], w1T).then_inc(z["s_wf"], 16)
                ac.dma_start(WR[rows, NCH:2 * NCH], w3T).then_inc(z["s_wf"], 16)
                ac.dma_start(WR[rows, 2 * NCH:WCOLS], routerT).then_inc(z["s_wf"], 16)
            ac.wait_ge(z["w2_zero"], 1)
            w2v = w2T.rearrange("(q two) h c -> two h q c", two=2)
            W2v = W2[:, :, :].rearrange("h (q k) c -> h k q c", k=3)
            a, m = CUT[1], HID - CUT[1]
            ac.dma_start(W2v[0:a, 0, :, 0:C], w2v[0, 0:a]).then_inc(z["s_w2"], 16)
            ac.dma_start(W2v[0:m, 1, :, 0:C], w2v[0, a:HID]).then_inc(z["s_w2"], 16)
            ac.dma_start(W2v[m:2 * m, 1, :, C:P], w2v[1, 0:m]).then_inc(z["s_w2"], 16)
            ac.dma_start(W2v[0:a, 2, :, C:P], w2v[1, m:HID]).then_inc(z["s_w2"], 16)
            ac.wait_ge(z["c_bias"], 1)

            def rsqrt(dst, src, tmp, scale, eps):
                link(ac.activation(tmp, src, ACT.Ln, bias=eps, scale=scale))
                return ac.activation(dst, tmp, ACT.Exp, bias=b_zero, scale=-0.5)

            def rsqrt_tiny(dst, src, tmp, rows=P):
                link(ac.activation(tmp, src, ACT.Ln, bias=b_zero[0:rows], scale=LN_SCALE))
                return ac.activation(dst, tmp, ACT.Exp, bias=b_20[0:rows], scale=-0.5)

            def a_copy(n):
                b, g = divmod(n, GROUPS)
                if g:
                    return
                ac.wait_ge(z["tok_done"], b + 1)
                for half in range(2):
                    rows = slice(C * half, C * half + C)
                    ac.activation(hfm[rows, :].rearrange("p (v k) -> p v k", k=NPATCH),
                                  bank[0][rows, :].rearrange("p (k v) -> p v k", k=NPATCH), ACT.Copy).then_inc(z["h_fm"], 1)
                ac.wait_ge(z["h_tp"], b + 1)
                ac.activation(H[:, TILES * b:TILES * b + 8, :].rearrange("p (h t) c -> p h t c", h=2),
                              bank[6][:, :].rearrange("p (t h c) -> p h t c", t=4, h=2), ACT.Copy).then_inc(z["h_copied"], 1)

            def a_rstd(n):
                ac.wait_ge(z["a_var"], n + 1)
                rsqrt(st[:, n, 12:15], st[:, n, 6:9], st[:, n, 9:12], 1 / C, b_eps5).then_inc(z["a_rstd"], 1)

            def a_xT(n):
                ac.wait_ge(z["a_tp"], n + 1)
                ac.activation(xnT[0:C, n, :], bank[1][0:C, 0:GW], ACT.Copy).then_inc(z["a_xT"], 1)

            def a_squares(n):
                if n == 0:
                    ac.wait_ge(z["c_ones"], 1)
                    ac.wait_ge(z["w_split"], 1)
                ac.wait_ge(z["a_qkv"], n + 1)
                if n >= 2:
                    ac.wait_ge(z["a_q2n"], n - 1)
                    ac.wait_ge(z["a_kv"], n - 1)
                qkv = wide[0][:, :, :].rearrange("p a b -> p (a b)").rearrange("p (t c) -> p t c", c=256)[:, 0:GT, :]
                ac.activation(QK2[:, n % 2, :, :, :].rearrange("p t a c -> p t (a c)"), qkv[:, :, 0:P], ACT.Square).then_inc(z["a_sqr"], 1)
                ac.activation(V1[:, n % 2, :, 0:C], qkv[:, :, P:192], ACT.Copy).then_inc(z["a_sqr"], 1)
                ac.wait_ge(z["a_n2"], n + 1)
                rsqrt_tiny(st[:, n, 33:36], st[:, n, 27:30], st[:, n, 30:33]).then_inc(z["a_rq"], 1)

            wave([a_copy, a_rstd, a_xT, a_squares, lambda n: None])

            for b in range(B):
                ac.wait_ge(z["p_c"], b + 1)
                rsqrt_tiny(kst[:, b, 2:3], kst[:, b, 0:1], kst[:, b, 1:2], C).then_inc(z["p_rc"], 1)

            def b_rstd(n):
                ac.wait_ge(z["b_var"], n + 1)
                rsqrt(st[:, n, 12:15], st[:, n, 6:9], st[:, n, 9:12], 1 / C, b_eps5).then_inc(z["b_rstd"], 1)
                ac.wait_ge(z["b_ms"], n + 1)
                rsqrt(st[:, n, 18:21], st[:, n, 15:18], st[:, n, 9:12], 1.0, b_eps6).then_inc(z["b_r1"], 1)

            def b_hT(n):
                ac.wait_ge(z["b_tp"], n + 1)
                ac.activation(hnT[:, n % 2, :], bank[1][0:C, 0:GW], ACT.Copy).then_inc(z["b_hT"], 1)

            def b_qk(n):
                ac.wait_ge(z["b_q"], n + 1)
                if n >= 2:
                    ac.wait_ge(z["b_hl"], n - 1)
                q = bank[0][:, 0:GT * P].rearrange("p (t c) -> p t c", c=P)
                ac.activation(QKs[:, n % 2, :, :, :].rearrange("p t h e -> p t (h e)"), q[:, :, 0:96], ACT.Copy).then_inc(z["b_qk"], 1)
                for r in range(GT):
                    ins = ac.activation(VA[:, GT * n + r, :, 0:HD], q[:, r, 96:128].rearrange("p (v e) -> p v e", e=HD), ACT.Copy)
                ins.then_inc(z["b_qk"], 1)

            def b_qT(n):
                for t in range(GT * n, GT * n + GT):
                    ac.wait_ge(z["b_qt"], t + 1)
                    src = (wide[0] if t % 2 == 0 else wide[1])[0:64, 0, :].rearrange("p (h q) -> p h q", h=NH)
                    ac.activation(QT[0:64, :, t * P:t * P + P], src, ACT.Copy).then_inc(z["b_qT"], 1)

            wave([b_rstd, b_hT, b_qk, b_qT])

            jj = 0
            for n in range(NG):
                g = n % GROUPS
                for j in range(GT * g + GT):
                    q0 = max(0, P * (j - GT * g))
                    for hp in range(2):
                        ac.wait_ge(z["st_done"], 2 * jj + hp + 1)
                        if jj >= PRING and hp == 0:
                            ac.wait_ge(z["pv_done"], jj - PRING + 1)
                        ac.activation(PR[:, jj % PRING, 2 * hp:2 * hp + 2, q0:GW], wide[hp][:, :, q0:GW], ACT.Exp,
                                      bias=b_zero, scale=HD ** -0.5).then_inc(z["e_done"], 1)
                    jj += 1
                ac.wait_ge(z["pv_done"], jj)
                if n >= 2:
                    ac.wait_ge(z["y_tp"], n - 1)
                ac.activation(YS[:, n % 2, :], bank[6][:, 0:GW], ACT.Copy).then_inc(z["y_cp"], 1)

            def w_yT(n):
                ac.wait_ge(z["w_tp"], n + 1)
                ac.activation(yT[:, n % 2, :], bank[0][0:C, 0:GW], ACT.Copy).then_inc(z["w_yT"], 1)

            def w_rs(n):
                ac.wait_ge(z["w_ss"], n + 1)
                rsqrt(st[:, n, 33:36], st[:, n, 27:30], st[:, n, 30:33], 1 / C, b_eps6).then_inc(z["w_rs"], 1)

            def w_fT(n):
                ac.wait_ge(z["w_ft"], n + 1)
                ac.activation(FT[:, n, :], bank[2][:, 0:GW], ACT.Copy).then_inc(z["w_fT"], 1)

            def w_exp(n):
                ac.wait_ge(z["w_lg"], n + 1)
                ac.activation(RL[:, tiles(n), :], RL[:, tiles(n), :], ACT.Exp, bias=b_zero).then_inc(z["w_e"], 1)

            wave([w_yT, w_rs, w_fT, w_exp])

            u = 0
            for n in range(NG):
                for c in range(CHUNKS):
                    m = chunk(c)[1]
                    ac.wait_ge(z["m_a"], u + 1)
                    if u >= 3:
                        ac.wait_ge(z["m_h"], u - 2)
                    ac.activation(SI[0:m, u % 3, :], bank[u % 2][0:m, 0:GW], ACT.Silu, bias=b_zero[0:m]).then_inc(z["m_s"], 1)
                    u += 1

        @block.vector
        def _(ve):
            link = linker(ve, z["ve_chain"])
            ve.memset(xnT[C:C + 1, :, :], 1.0)
            ve.memset(QT[64:66, :, :].bitcast(F32), 0.0)
            ve.memset(KT[64:66, :, :].bitcast(F32), 1.0).then_inc(z["w_small"], 1)
            ve.wait_ge(z["g_ready"], 1)
            for h in range(2):
                src = wide[0][64 * h:64 * h + 64, :, :].rearrange("p a (o j h r) -> p h j r (a o)", o=32, j=2, h=2)[:, h]
                for j in range(2):
                    ins = ve.tensor_copy(G[64 * h:64 * h + 64, j, :, :], src[:, j])
            ins.then_inc(z["g_done"], 1)
            ve.wait_ge(z["s_wa"], 16 * 8)
            qk = Wqkv[:, 0:P].rearrange("p (a c) -> p a c", a=2)
            link(ve.tensor_reduce(wmean[:, :], qk, AX.X, ALU.add))
            link(ve.tensor_scalar(wmean[:, :], wmean[:, :], -1 / C, None, ALU.mult))
            ve.tensor_tensor(qk, qk, bc(wmean[:, :], [C + 1, 2, C]), ALU.add)
            ve.tensor_scalar(Wffn[:, :], Wffn[:, :], ln1_sb[:, 0:1], None, ALU.mult).then_inc(z["w_small"], 1)
            ve.wait_ge(z["wvo_ready"], 1)
            ve.tensor_tensor(WVO[:, :], bank[6][0:C + 1, P:P + C], bout[:, :], ALU.add).then_inc(z["wvo_done"], 1)

            def mean(n, sem_):
                link(ve.tensor_reduce(st[:, n, 0:3], H[:, tiles(n), :], AX.X, ALU.add))
                ve.tensor_scalar(st[:, n, 3:6], st[:, n, 0:3], -1 / C, None, ALU.mult).then_inc(sem_, 1)

            def a_stats(n):
                ve.wait_ge(z["h_copied"], n // GROUPS + 1)
                if n % GROUPS == GROUPS - 1:
                    ve.wait_ge(z["s_txt"], 16 * B)
                mean(n, z["a_mean"])
                ve.wait_ge(z["a_sq"], n + 1)
                ve.tensor_reduce(st[:, n, 6:9], SQ[:, n % 2, :, :], AX.X, ALU.add).then_inc(z["a_var"], 1)

            def a_norms(n):
                r = st[:, n, 21:27]
                ve.wait_ge(z["a_sqr"], 2 * n + 2)
                link(ve.tensor_reduce(st[:, n, 15:21], QK2[:, n % 2, :, :, :].rearrange("p t a c -> p (t a) c"), AX.X, ALU.add))
                link(ve.tensor_scalar(r, st[:, n, 15:21], 1e-7, None, ALU.add))
                link_r = ve.reciprocal(r, r)
                link_r.then_inc(z["a_r"], 1)
                ve.wait_ge(z["a_r"], n + 1)
                rq = r.rearrange("p (t two) -> p t two", two=2)[:, :, 0]
                ve.wait_ge(z["a_q4"], n + 1)
                link(ve.tensor_reduce(st[:, n, 27:30], Q4[:, n % 2, :, :], AX.X, ALU.add))
                link(ve.tensor_tensor(st[:, n, 27:30], st[:, n, 27:30], rq, ALU.mult))
                link(ve.tensor_tensor(st[:, n, 27:30], st[:, n, 27:30], rq, ALU.mult))
                ve.tensor_scalar(st[:, n, 27:30], st[:, n, 27:30], 1e-24, None, ALU.max).then_inc(z["a_n2"], 1)
                ve.wait_ge(z["a_rq"], n + 1)
                ve.tensor_tensor(st[:, n, 36:39], st[:, n, 33:36], rq, ALU.mult).then_inc(z["a_f"], 1)

            def a_q2T(n):
                ve.wait_ge(z["a_q2tp"], n + 1)
                ve.tensor_copy(q2T[:, n, :], bank[7][0:C, 0:GW]).then_inc(z["a_q2T"], 1)

            wave([lambda n: None, a_stats, lambda n: None, a_norms, a_q2T])

            for b in range(B):
                ve.wait_ge(z["a_kv"], GROUPS * (b + 1))
                ve.tensor_scalar(kst[:, b, 0:1], bank[4 + b][C:P, C:C + 1], 1e-24, None, ALU.max).then_inc(z["p_c"], 1)
                ve.wait_ge(z["p_rc"], b + 1)
                ve.tensor_scalar(KVS[:, b, :], bank[4 + b][0:C, 0:C], kst[:, b, 2:3], L ** -0.5, ALU.mult, ALU.mult).then_inc(z["p_kvs"], 1)
                ve.wait_ge(z["p_tp"], b + 1)
                ve.tensor_copy(KVST[:, b, :], bank[6][0:C, 0:C]).then_inc(z["p_kvT"], 1)
                ve.wait_ge(z["p_kvo"], b + 1)
                ve.tensor_copy(KVO[:, b, :], bank[6][0:C, C:P]).then_inc(z["p_kvoS"], 1)

            def b_stats(n):
                ve.wait_ge(z["b_o"], n + 1)
                ins = ve.tensor_tensor(H[:, tiles(n), :], H[:, tiles(n), :], bank[6][:, 0:GT * C].rearrange("p (t c) -> p t c", c=C), ALU.add)
                ins.then_inc(z["b_h1"], 1)
                ve.wait_ge(z["b_h1"], n + 1)
                mean(n, z["b_mean"])
                ve.wait_ge(z["b_sq"], n + 1)
                ve.tensor_reduce(st[:, n, 6:9], SQ[:, n % 2, :, :], AX.X, ALU.add).then_inc(z["b_var"], 1)
                ve.wait_ge(z["b_rstd"], n + 1)
                link(ve.tensor_tensor(st[:, n, 15:18], st[:, n, 12:15], st[:, n, 12:15], ALU.mult))
                ve.scalar_tensor_tensor(out=st[:, n, 15:18], in0=st[:, n, 15:18], scalar=1 / C, in1=st[:, n, 6:9],
                                        op0=ALU.mult, op1=ALU.mult).then_inc(z["b_ms"], 1)

            def b_kT(n):
                for t in range(GT * n, GT * n + GT):
                    ve.wait_ge(z["b_qt"], t + 1)
                    src = (wide[0] if t % 2 == 0 else wide[1])[0:64, 1, 0:NKV * P].rearrange("p (h q) -> p h q", h=NKV)
                    ve.tensor_copy(KT[0:64, :, t * P:t * P + P], src).then_inc(z["b_kT"], 1)

            wave([b_stats, lambda n: None, lambda n: None, b_kT])

            unit = [0]

            def maxima(t):
                nch = s1_chunks(t)
                for h, k, w, _ in s1_units(t):
                    u = unit[0]
                    unit[0] += 1
                    ve.wait_ge(z["s_done"], u + 1)
                    ins = ve.tensor_reduce(MXC[:, t, h, k // 512:k // 512 + 1], bank[u % 2][:, 0:w], AX.X, ALU.max, negate=True)
                    ins.then_inc(z["s_max"], 1)
                ve.wait_ge(z["s_max"], unit[0])
                ve.tensor_reduce(NM[:, t, :], MXC[:, t, :, 0:nch], AX.X, ALU.min).then_inc(z["s_nm"], 1)

            def copy_max(t):
                ve.wait_ge(z["s_mt"], t + 1)
                ve.tensor_copy(QT[64:66, :, t * P:t * P + P], bank[7][0:2, :].rearrange("p (h q) -> p h q", h=NH)).then_inc(z["s_mT"], 1)

            def outputs(n):
                ve.wait_ge(z["y_tp"], n + 1)
                y = bank[7][:, 0:GT * P].rearrange("p (t h e) -> p t h e", t=GT, h=NH)
                rs = st[:, n, 40:52].rearrange("p (t h) -> p t h", t=GT)
                link(ve.reciprocal(rs, y[:, :, :, HD]))
                ve.tensor_tensor(YN[:, tiles(n), :, :], y[:, :, :, 0:HD], bc(rs, [P, GT, NH, HD]), ALU.mult).then_inc(z["y_n"], 1)

            for t in range(GT):
                maxima(t)
                copy_max(t)
            for n, j, finished, begun in attention_steps():
                if finished is not None:
                    copy_max(finished)
                if begun is not None:
                    maxima(begun)
                if j is None:
                    outputs(n)

            def w_x2(n):
                ve.wait_ge(z["w_o"], n + 1)
                ve.tensor_tensor(D[:, tiles(n), :], D[:, tiles(n), :], bank[1][:, 0:GT * C].rearrange("p (t c) -> p t c", c=C), ALU.add).then_inc(z["w_x2"], 1)
                ve.wait_ge(z["w_sq"], n + 1)
                ve.tensor_reduce(st[:, n, 27:30], SQ[:, n % 2, :, :], AX.X, ALU.add).then_inc(z["w_ss"], 1)

            def w_route(n):
                t3 = tiles(n)
                ve.wait_ge(z["w_r"], n + 1)
                lg = bank[3][:, 0:GT * NE].rearrange("p (t e) -> p t e", e=NE)
                link(ve.tensor_reduce(st[:, n, 52:55], lg, AX.X, ALU.max, negate=True))
                ve.tensor_tensor(RL[:, t3, :], lg, bc(st[:, n, 52:55], [P, GT, NE]), ALU.add).then_inc(z["w_lg"], 1)
                ve.wait_ge(z["w_e"], n + 1)
                ve.tensor_reduce(st[:, n, 55:58], RL[:, t3, :], AX.X, ALU.add)
                for t in range(GT * n, GT * n + GT):
                    ins = ve.max(TOP[:, t, :], RL[:, t, :])
                link(ins)
                for t in range(GT * n, GT * n + GT):
                    ins = ve.max_index(IDX[:, t, :], TOP[:, t, :], RL[:, t, :])
                link(ins)
                ve.tensor_copy(IDF[:, t3, :], IDX[:, t3, 0:2])
                link(ve.tensor_tensor(st[:, n, 58:61], TOP[:, t3, 0], TOP[:, t3, 1], ALU.add))
                link(ve.scalar_tensor_tensor(out=st[:, n, 58:61], in0=st[:, n, 55:58], scalar=1e-9, in1=st[:, n, 58:61],
                                             op0=ALU.mult, op1=ALU.add))
                link(ve.reciprocal(st[:, n, 58:61], st[:, n, 58:61]))
                for t in range(GT * n, GT * n + GT):
                    ve.tensor_scalar(WA[:, t, :], iota, IDF[:, t, 0:1], TOP[:, t, 0:1], ALU.is_equal, ALU.mult)
                    ins = ve.tensor_scalar(WB[:, t, :], iota, IDF[:, t, 1:2], TOP[:, t, 1:2], ALU.is_equal, ALU.mult)
                link(ins)
                link(ve.tensor_tensor(WA[:, t3, :], WA[:, t3, :], WB[:, t3, :], ALU.add))
                ve.tensor_tensor(WA[:, t3, :], WA[:, t3, :], bc(st[:, n, 58:61], [P, GT, NE]), ALU.mult).then_inc(z["w_wt"], 1)

            wave([lambda n: None, w_x2, lambda n: None, w_route])
            ve.wait_ge(z["w_wt"], NG)

            u = 0
            for n in range(NG):
                for c in range(CHUNKS):
                    m = chunk(c)[1]
                    ve.wait_ge(z["m_s"], u + 1)
                    ve.wait_ge(z["m_b"], u + 1)
                    if u >= 3:
                        ve.wait_ge(z["m_y"], u - 2)
                    ve.tensor_tensor(HH[0:m, u % 3, :], SI[0:m, u % 3, :], bank[2 + u % 2][0:m, 0:GW], ALU.mult).then_inc(z["m_h"], 1)
                    u += 1
                for r in range(GT):
                    t = GT * n + r
                    ve.wait_ge(z["m_y"], CHUNKS * (n + 1))
                    if t >= 3:
                        ve.wait_ge(z["m_tr"], t - 2)
                    ve.tensor_tensor(YW[:, t % 3], bank[4 + r][:, :].rearrange("p (e c) -> p e c", c=C), bc(WA[:, t, :], [P, NE, C]), ALU.mult).then_inc(z["m_yw"], 1)

        @block.tensor
        def _(pe):
            pe.wait_ge(z["s_wtok"], 32)
            for o in range(C):
                for h in range(2):
                    ins = pe.matmul(bank[2 + o // 32][64 * h:64 * h + 64, (o % 32) * PATCH:(o % 32 + 1) * PATCH], Wt[:, o, :], dft_sb[:, :],
                                    start=True, stop=True, tile_position=(0, 64 * h))
            ins.then_inc(z["g_ready"], 1)
            pe.wait_ge(z["w_small"], 2)
            pe.matmul(bank[6][0:C + 1, P:P + C], WvT[:, :], Wout[:, :], start=True, stop=True).then_inc(z["wvo_ready"], 1)
            pe.wait_ge(z["wvo_done"], 1)
            pe.wait_ge(z["s_cst"], 16)
            pe.wait_ge(z["g_done"], 1)

            def a_tok(n):
                b, g = divmod(n, GROUPS)
                if g:
                    return
                if g == 0:
                    pe.wait_ge((z["s_x0"], z["s_x1"])[b], 16 * (2 + 2 * RUN))
                if b:
                    pe.wait_ge(z["h_fm"], 2 * b)
                taps = [(j, q) for j in range(2) for q in range(RUN)]
                for i, (j, q) in enumerate(taps):
                    for half in range(2):
                        xs = X[:, b, j:j + NPATCH, q, V // 2 * half:V // 2 * half + V // 2]
                        ins = pe.matmul(bank[0][C * half:C * half + C, :], G[:, j, q, :], xs, start=(i == 0), stop=(i == 2 * RUN - 1),
                                        tile_position=(0, C * half))
                ins.then_inc(z["tok_done"], 1)
                pe.wait_ge(z["h_fm"], 2 * b + 2)
                if b:
                    pe.wait_ge(z["h_copied"], b)
                for t in range(4):
                    ins = pe.transpose(bank[6][:, P * t:P * t + P], hfm[:, P * t:P * t + P], ident)
                ins.then_inc(z["h_tp"], 1)

            def transpose_group(dst, src, sem_):
                for r in range(GT):
                    ins = pe.transpose(dst[0:C, P * r:P * r + P], src(r), ident)
                ins.then_inc(sem_, 1)

            def a_tp(n):
                pe.wait_ge(z["a_xn"], n + 1)
                if n:
                    pe.wait_ge(z["a_xT"], n)
                transpose_group(bank[1], lambda r: D[:, GT * n + r, :], z["a_tp"])

            def a_qkv(n):
                pe.wait_ge(z["a_xT"], n + 1)
                if n:
                    pe.wait_ge(z["a_sqr"], 2 * n)
                for r in range(GT):
                    ins = pe.matmul(wide[0][:, r // 2, 256 * (r % 2):256 * (r % 2) + 192], xnT[:, n, P * r:P * r + P], Wqkv[:, :], start=True, stop=True)
                ins.then_inc(z["a_qkv"], 1)

            def a_kv(n):
                b, g = divmod(n, GROUPS)
                pe.wait_ge(z["a_kk"], n + 1)
                for r in range(GT):
                    kk = KK[:, n % 2, r, :, :].rearrange("p a c -> p (a c)")
                    ins = pe.matmul(bank[4 + b][:, 0:C + 1], kk, V1[:, n % 2, r, :], start=(g == 0 and r == 0), stop=(g == GROUPS - 1 and r == GT - 1))
                ins.then_inc(z["a_kv"], 1)
                pe.wait_ge(z["a_q2n"], n + 1)
                if n:
                    pe.wait_ge(z["a_q2T"], n)
                transpose_group(bank[7], lambda r: Q2[:, n % 2, r, :], z["a_q2tp"])

            wave([a_tok, lambda n: None, a_tp, a_qkv, a_kv])

            for b in range(B):
                pe.wait_ge(z["p_kvs"], b + 1)
                pe.transpose(bank[6][0:C, 0:C], KVS[:, b, :], ident[0:C, 0:C]).then_inc(z["p_tp"], 1)
                pe.wait_ge(z["p_kvT"], b + 1)
                pe.matmul(bank[6][0:C, C:P], KVST[:, b, :], Wout[:, :], start=True, stop=True).then_inc(z["p_kvo"], 1)

            def b_out_(n):
                pe.wait_ge(z["p_kvoS"], B)
                pe.wait_ge(z["a_q2T"], n + 1)
                if n:
                    pe.wait_ge(z["b_h1"], n)
                for r in range(GT):
                    o = bank[6][:, C * r:C * r + C]
                    pe.matmul(o, xnT[:, n, P * r:P * r + P], WVO[:, :], start=True, stop=False)
                    ins = pe.matmul(o, q2T[:, n, P * r:P * r + P], KVO[:, n // GROUPS, :], start=False, stop=True)
                ins.then_inc(z["b_o"], 1)

            def b_tp(n):
                pe.wait_ge(z["b_hn"], n + 1)
                if n:
                    pe.wait_ge(z["b_hT"], n)
                transpose_group(bank[1], lambda r: HN[:, n % 2, r, :], z["b_tp"])

            def b_q(n):
                pe.wait_ge(z["b_hT"], n + 1)
                if n:
                    pe.wait_ge(z["b_qk"], 2 * n)
                for r in range(GT):
                    ins = pe.matmul(bank[0][:, P * r:P * r + P], hnT[:, n % 2, P * r:P * r + P], Wffn[:, :], start=True, stop=True)
                ins.then_inc(z["b_q"], 1)

            def b_qt(n):
                pe.wait_ge(z["b_hl"], n + 1)
                for t in range(GT * n, GT * n + GT):
                    if t >= 2:
                        pe.wait_ge(z["b_qT"], t - 1)
                        pe.wait_ge(z["b_kT"], t - 1)
                    w = wide[t % 2]
                    src = HL[:, n % 2, t % GT, :, :, :].bitcast(F32)
                    for h in range(NH):
                        pe.transpose(w[0:64, 0, P * h:P * h + P], src[:, h].rearrange("p a e -> p (a e)"), ident)
                    for h in range(NKV):
                        ins = pe.transpose(w[0:64, 1, P * h:P * h + P], src[:, NH + h].rearrange("p a e -> p (a e)"), ident)
                    ins.then_inc(z["b_qt"], 1)

            wave([b_out_, b_tp, b_q, b_qt])

            pe.wait_ge(z["c_bf"], 2)
            pe.wait_ge(z["b_qT"], NT)
            pe.wait_ge(z["b_kT"], NT)
            unit = [0]
            misc = [0]

            def misc_bank():
                if misc[0]:
                    pe.wait_ge(z["misc_free"], misc[0])
                misc[0] += 1

            def scores_for_max(t):
                b = t // TILES
                for h, k, w, diag in s1_units(t):
                    u = unit[0]
                    unit[0] += 1
                    if u >= 2:
                        pe.wait_ge(z["s_max"], u - 1)
                    o = bank[u % 2]
                    k0 = b * L + k
                    ins = pe.matmul(o[:, 0:w], QT[:, h, t * P:t * P + P], KT[:, h // 2, k0:k0 + w], start=True, stop=not diag)
                    if diag:
                        ins = pe.matmul(o[:, w - P:w], identb[:, :], maskb[:, :], start=False, stop=True)
                    ins.then_inc(z["s_done"], 1)

            def transpose_max(t):
                pe.wait_ge(z["s_ml"], t + 1)
                if t:
                    pe.wait_ge(z["s_mT"], t)
                done = outs[0]
                if done:
                    pe.wait_ge(z["y_n"], done)
                for h in range(NH):
                    ins = pe.transpose(bank[7][0:2, P * h:P * h + P], ML[:, t, h, :].bitcast(F32), ident)
                ins.then_inc(z["s_mt"], 1)

            outs = [0]
            jj = [0]

            def scores(n, j):
                g = n % GROUPS
                q0 = max(0, P * (j - GT * g))
                key = (n // GROUPS) * L + P * j
                for hp in range(2):
                    if jj[0] >= 1:
                        pe.wait_ge(z["e_done"], 2 * jj[0] - 1 + hp)
                    for hh in range(2):
                        ins = pe.matmul(wide[hp][:, hh, q0:GW], KT[:, hp, key:key + P], QT[:, 2 * hp + hh, GW * n + q0:GW * n + GW], start=True, stop=True)
                    ins.then_inc(z["st_done"], 1)
                jj[0] += 1

            diags = [0]

            def weigh(n, j, i):
                g = n % GROUPS
                q0 = max(0, P * (j - GT * g))
                pe.wait_ge(z["e_done"], 2 * i + 2)
                if j >= GT * g:
                    diags[0] += 1
                    pe.wait_ge(z["m_done"], diags[0])
                for h in range(NH):
                    ins = pe.matmul(bank[6][32 * h:32 * h + 32, q0:GW], VA[:, (n // GROUPS) * TILES + j, h // 2, :],
                                    PR[:, i % PRING, h, q0:GW], start=(j == 0), stop=(j == GT * g + GT - 1), tile_position=(0, 32 * h))
                ins.then_inc(z["pv_done"], 1)

            for t in range(GT):
                scores_for_max(t)
                transpose_max(t)
            for n, j, finished, begun in attention_steps():
                if j == 0:
                    pe.wait_ge(z["s_mT"], GT * n + GT)
                    if n:
                        pe.wait_ge(z["y_cp"], n)
                if j is not None:
                    scores(n, j)
                    if finished is not None:
                        transpose_max(finished)
                    if begun is not None:
                        scores_for_max(begun)
                    if j:
                        weigh(n, j - 1, jj[0] - 2)
                    continue
                weigh(n, GT * (n % GROUPS) + GT - 1, jj[0] - 1)
                if finished is not None:
                    transpose_max(finished)
                    pe.wait_ge(z["s_mT"], finished + 1)
                pe.wait_ge(z["y_cp"], n + 1)
                if n:
                    pe.wait_ge(z["y_n"], n)
                for r in range(GT):
                    ins = pe.transpose(bank[7][:, P * r:P * r + P], YS[:, n % 2, P * r:P * r + P], ident)
                ins.then_inc(z["y_tp"], 1)
                outs[0] += 1

            def w_tp(n):
                pe.wait_ge(z["y_n"], n + 1)
                if n:
                    pe.wait_ge(z["w_yT"], n)
                transpose_group(bank[0], lambda r: YN[:, GT * n + r, :, :].rearrange("p h e -> p (h e)"), z["w_tp"])

            def w_o(n):
                pe.wait_ge(z["w_yT"], n + 1)
                if n:
                    pe.wait_ge(z["w_x2"], n)
                for r in range(GT):
                    ins = pe.matmul(bank[1][:, C * r:C * r + C], yT[:, n % 2, P * r:P * r + P], WoT[:, :], start=True, stop=True)
                ins.then_inc(z["w_o"], 1)

            def w_ft(n):
                pe.wait_ge(z["w_fl"], n + 1)
                if n:
                    pe.wait_ge(z["w_fT"], n)
                for r in range(GT):
                    src = FL[:, n % 2, r, :, :].bitcast(F32).rearrange("p a c -> p (a c)")
                    ins = pe.transpose(bank[2][:, P * r:P * r + P], src, ident)
                ins.then_inc(z["w_ft"], 1)

            def w_r(n):
                if n == 0:
                    pe.wait_ge(z["w_split"], 1)
                pe.wait_ge(z["w_fT"], n + 1)
                if n:
                    pe.wait_ge(z["w_lg"], n)
                for r in range(GT):
                    for w, first in ((WH, True), (WL, False)):
                        ins = pe.matmul(bank[3][:, NE * r:NE * r + NE], FT[:, n, P * r:P * r + P], w[:, 2 * NCH:WCOLS], start=first, stop=not first)
                ins.then_inc(z["w_r"], 1)

            wave([w_tp, w_o, w_ft, w_r])

            pe.wait_ge(z["s_w2"], 64)
            pe.wait_ge(z["w_lg"], NG)

            def hidden(n, c, u):
                c0, m = chunk(c)
                for k, (base, dst, sem_) in enumerate(((0, bank[u % 2], z["m_a"]), (NCH, bank[2 + u % 2], z["m_b"]))):
                    if u >= 2:
                        pe.wait_ge((z["m_s"], z["m_h"])[k], u - 1)
                    for w, first in ((WH, True), (WL, False)):
                        ins = pe.matmul(dst[0:m, 0:GW], w[:, base + c0:base + c0 + m], FT[:, n, :], start=first, stop=not first)
                    ins.then_inc(sem_, 1)

            def combine(n, c, u):
                m = chunk(c)[1]
                pair, k = divmod(c, 3)
                lo, hi = ((0, C), (0, P), (C, P))[k]
                pe.wait_ge(z["m_h"], u + 1)
                if c == 0 and n:
                    pe.wait_ge(z["m_yw"], GT * n)
                for r in range(GT):
                    ins = pe.matmul(bank[4 + r][:, P * pair + lo:P * pair + hi], HH[0:m, u % 3, P * r:P * r + P], W2[0:m, c, lo:hi],
                                    start=(c == 0), stop=(c == CHUNKS - 1), skip_group_check=True)
                ins.then_inc(z["m_y"], 1)

            todo = [(n, c, CHUNKS * n + c) for n in range(NG) for c in range(CHUNKS)]
            for i, item in enumerate(todo):
                hidden(*item)
                if i:
                    combine(*todo[i - 1])
            combine(*todo[-1])


def kernel(x, txt, L0_tok_W, L0_attn_W_qkv, L0_attn_b_qkv, L0_attn_W_out, L0_attn_b_out, L0_ffn_ln1_w, L0_ffn_ln2_w,
           L0_ffn_wq, L0_ffn_wk, L0_ffn_wv, L0_ffn_wo, L0_ffn_router_w, L0_ffn_w1, L0_ffn_w2, L0_ffn_w3):
    import numpy as np
    import concourse.bacc as bacc
    from concourse.bass_utils import run_bass_kernel_spmd

    c = np.ascontiguousarray
    f = np.arange(PATCH // 2 + 1)[:, None] * np.arange(PATCH)[None, :] * (2 * np.pi / PATCH)
    dft = np.concatenate([np.cos(f), -np.sin(f)]) / np.sqrt(PATCH)
    inv = 1.0 / 10000.0 ** (np.arange(0, HD, 2, dtype=np.float32) / HD)
    angle = np.outer(np.arange(L, dtype=np.float32), inv)
    table = lambda a, b: np.concatenate([a, b], axis=1).reshape(TILES, P, HD).transpose(1, 0, 2).reshape(P, TILES * HD)
    consts = np.concatenate([np.eye(P), table(np.cos(angle), np.cos(angle)), table(-np.sin(angle), np.sin(angle)),
                             np.tile(np.arange(NE), (P, 1))], axis=1)
    flatT = lambda w: c(w.reshape(NCH, C).T)
    arrays = {
        "x": c(x), "txt": c(txt),
        "w_tok": c(L0_tok_W.reshape(C, NF, C).transpose(1, 0, 2)),
        "w_qkv": c(L0_attn_W_qkv), "b_qkv": c(L0_attn_b_qkv.reshape(1, 3 * C)),
        "w_vT": c(np.concatenate([L0_attn_W_qkv[:, 2 * C:], L0_attn_b_qkv[None, 2 * C:]]).T),
        "w_out": c(L0_attn_W_out), "b_out": c(L0_attn_b_out.reshape(1, C)),
        "ln1": c(L0_ffn_ln1_w.reshape(C, 1)), "ln2": c(L0_ffn_ln2_w.reshape(C, 1)),
        "w_ffn": c(np.concatenate([L0_ffn_wq, L0_ffn_wk, L0_ffn_wv]).T),
        "woT": c(L0_ffn_wo.T), "routerT": c(L0_ffn_router_w.T),
        "w1T": flatT(L0_ffn_w1), "w3T": flatT(L0_ffn_w3), "w2T": c(L0_ffn_w2.transpose(0, 2, 1)),
        "dft": dft.astype(np.float32), "consts": consts.astype(np.float32),
    }
    nc = bacc.Bacc("TRN2", target_bir_lowering=False, num_devices=1)
    args = {n: nc.dram_tensor(f"in_{n}", a.shape, F32, kind="ExternalInput").ap() for n, a in arrays.items()}
    out = nc.dram_tensor("out_h", [B, L, C], F32, kind="ExternalOutput").ap()
    build(nc, out=out, **args)
    r = run_bass_kernel_spmd(nc, [{f"in_{n}": a for n, a in arrays.items()}], core_ids=[0])
    return r.results[0]["out_h"]
```

```python
from contextlib import ExitStack

import concourse.bass as bass
from concourse import mybir

F32 = mybir.dt.float32
F32R = mybir.dt.float32r
BF16 = mybir.dt.bfloat16
U32 = mybir.dt.uint32
ALU = mybir.AluOpType
ACT = mybir.ActivationFunctionType
AX = mybir.AxisListType

P = 128
B, C, T, V = 2, 64, 128, 64
PATCH, STRIDE = 16, 8
NBLK = T // STRIDE + 1
NPATCH = T // STRIDE
NF = 2 * (PATCH // 2 + 1)
RUN = 4
TOK = V * NPATCH
TXT = 128
L = TOK + TXT
TILES = L // P
GT = 3
GROUPS = TILES // GT
NG = B * GROUPS
NT = B * TILES
GW = GT * P
NH, NKV, HD = 4, 2, 16
NE, HID = 8, 170
NCH = NE * HID
PAIRS = NE // 2
CUT = (0, 114, 226, 340)
CHUNKS = PAIRS * 3
HIDP = 114
WCOLS = 2 * NCH + NE
LN_SCALE = 2.0 ** 40
LN2_20 = 20 * 0.6931471805599453
NEG = -1e30
PRING = 4


def chunk(c):
    return (c // 3) * 2 * HID + CUT[c % 3], CUT[c % 3 + 1] - CUT[c % 3]


def s1_units(tile):
    n = (tile % TILES + 1) * P
    return [(h, k, min(512, n - k), k + 512 >= n) for k in range(0, n, 512) for h in range(NH)]


def s1_chunks(tile):
    return -(-(tile % TILES + 1) * P // 512)


def wave(groups, stages):
    return [(stages[k], groups[s - k]) for s in range(len(groups) + len(stages) - 1)
            for k in reversed(range(len(stages))) if 0 <= s - k < len(groups)]


def merged(main, side):
    order = [((i + 0.5) / len(main), 0, item) for i, item in enumerate(main)]
    order += [((i + 0.5) / len(side), 1, item) for i, item in enumerate(side)]
    return [item for _, _, item in sorted(order, key=lambda x: x[:2])]


def maxima_items(tiles):
    items, waiting = [], []
    for t in tiles:
        units = len(s1_units(t))
        for i in range(units):
            items.append(("max", t, i))
            if i == units // 2 and waiting:
                items.append(("max_row", waiting.pop()))
        waiting.append(t)
    return items + [("max_row", t) for t in waiting]


def attention_items(n, side):
    steps = GT * (n % GROUPS) + GT
    items = []
    for j in range(steps):
        items += [("score", n, j, h) for h in range(NH)]
        if j:
            items.append(("weigh", n, j - 1))
    items += [("weigh", n, steps - 1), ("y_copy", n), ("y_turn", n)]
    return merged(items, side)


def plan():
    g = [list(range(GROUPS * b, GROUPS * b + GROUPS)) for b in range(B)]
    stages_a = ["a_stats", "a_norm", "a_qkv", "a_sums", "a_kv"]
    stages_b = ["b_out", "b_norm", "b_turn", "b_qkv", "b_rope", "b_split", "b_qk"]
    stages_w = ["w_turn", "w_out", "w_norm", "w_split", "w_route"]
    tiles = [list(range(GT * n, GT * n + GT)) for n in range(NG)]
    order = [("tokens", 0)] + wave(g[0], stages_a) + [("kv", 0), ("tokens", 1)] + wave(g[0], stages_b)
    order += maxima_items(tiles[0])
    side = wave(g[1], stages_a) + [("kv", 1)] + wave(g[1], stages_b)
    first = attention_items(0, maxima_items(tiles[1])) + attention_items(1, maxima_items(tiles[2])) + attention_items(2, [])
    order += merged(first, side)
    order += maxima_items(tiles[3])
    order += attention_items(3, maxima_items(tiles[4])) + attention_items(4, maxima_items(tiles[5]))
    order += attention_items(5, wave(g[0], stages_w))
    return order + wave(g[1], stages_w)


def build(nc, x, txt, w_tok, qkv_w, qkv_b, w_vT, out_w, out_b, ln1, ln2, w_ffn, woT, routerT, w1T, w3T, w2T, dft, consts, out):
    with ExitStack() as ctx:
        def sb(name, shape, dt=F32):
            return ctx.enter_context(nc.sbuf_tensor(name, shape, dt))

        def sem(name):
            return ctx.enter_context(nc.semaphore(name))

        X = sb("X", [P, B, NBLK, RUN, V])
        early = sb("early", [P, 2 * NG * GW])
        Wt = early[0:NF, 0:C * C].rearrange("p (o c) -> p o c", c=C)
        xnT = early[0:C + 1, 0:NG * GW].rearrange("p (n q) -> p n q", n=NG)
        q2T = early[0:C, NG * GW:2 * NG * GW].rearrange("p (n q) -> p n q", n=NG)
        work = sb("work", [P, 16 * GT * C])
        WR = work[:, 0:WCOLS]
        cut = lambda first, k, pat, **kw: work[:, first * GT * C:(first + 2 * k) * GT * C].rearrange(pat, s=2, c=C, **kw)
        SQ = cut(0, 1, "p (s t c) -> p s t c", t=GT)
        QK2 = cut(2, 2, "p (s t a c) -> p s t a c", t=GT, a=2)
        Q4 = cut(6, 1, "p (s t c) -> p s t c", t=GT)
        KK = cut(8, 2, "p (s t a c) -> p s t a c", t=GT, a=2)
        Q2 = cut(12, 1, "p (s t c) -> p s t c", t=GT)
        HN = cut(14, 1, "p (s t c) -> p s t c", t=GT)
        WH = sb("WH", [P, WCOLS], F32R)
        WL = sb("WL", [P, WCOLS], F32R)
        W2 = sb("W2", [HIDP, CHUNKS, P])
        G = sb("G", [P, 2, RUN, 64])
        dft_sb = sb("dft_sb", [NF, PATCH])
        cst = sb("cst", [P, 128 + 2 * TILES * HD + NE])
        ident = cst[:, 0:128]
        cos = cst[:, 128:128 + TILES * HD].rearrange("p (t e) -> p t e", e=HD)
        sin = cst[:, 128 + TILES * HD:128 + 2 * TILES * HD].rearrange("p (t e) -> p t e", e=HD)
        iota = cst[:, 128 + 2 * TILES * HD:128 + 2 * TILES * HD + NE]
        identb = sb("identb", [P, P], BF16)
        maskb = sb("maskb", [P, P], BF16)
        bias = sb("bias", [P, 5])
        b_eps5, b_eps6, b_zero, b_20, b_eps11 = (bias[:, i:i + 1] for i in range(5))
        ln1_sb = sb("ln1_sb", [C, 1])
        ln2_sb = sb("ln2_sb", [P, 1])
        Wqkv = sb("Wqkv", [C + 1, 192])
        wmean = sb("wmean", [C + 1, 2])
        WvT = sb("WvT", [C, C + 1])
        Wout = sb("Wout", [C, C])
        bout = sb("bout", [C + 1, C])
        WVO = sb("WVO", [C + 1, C])
        KVS = sb("KVS", [C, B, C])
        KVST = sb("KVST", [C, B, C])
        KVO = sb("KVO", [C, B, C])
        Wffn = sb("Wffn", [C, P])
        WoT = sb("WoT", [C, C])
        st = sb("st", [P, NG, 64])
        kst = sb("kst", [C, B, 4])
        KVA = sb("KVA", [P, B, C + 1])
        BN = sb("BN", [P, NG, GT, 6])
        MV = sb("MV", [P, NG, GT, 2])
        H = sb("H", [P, NT, C])
        D = sb("D", [P, NT, C])
        V1 = sb("V1", [P, 2, GT, C + 1])
        feat = sb("feat", [P, 2, GW])
        hfm = feat[:, :, :].rearrange("p s q -> p (s q)")[:, 0:TOK // 2]
        hnT = feat[0:C, :, :]
        yT = feat[0:C, :, :]
        QKs = sb("QKs", [P, 2, GT, 6, HD])
        RT = sb("RT", [P, 2, 2, GT, 6, HD])
        HL = sb("HL", [P, 2, GT, 6, 4, HD], F32R)
        QT = sb("QT", [P, NH, NT * P], F32R)
        KT = sb("KT", [P, NKV, NT * P], F32R)
        VA = sb("VA", [P, NT, NKV, 32])
        MXC = sb("MXC", [P, NT, NH, 3])
        NM = sb("NM", [P, NT, NH])
        ML = sb("ML", [P, NT, NH, 2], F32R)
        Xf = X[:, :, :, :, :].rearrange("p b k r v -> p (b k r v)")
        PR = Xf[:, 0:PRING * NH * GW].rearrange("p (s h q) -> p s h q", s=PRING, h=NH)
        yo = PRING * NH * GW
        YS = Xf[:, yo:yo + 2 * GW].rearrange("p (s q) -> p s q", s=2)
        YN = Xf[:, yo + 2 * GW:yo + 2 * GW + NT * C].rearrange("p (t h e) -> p t h e", h=NH, e=HD)
        FL = sb("FL", [P, 2, GT, 2, C], F32R)
        FT = sb("FT", [P, NG, GW], F32R)
        RL = sb("RL", [P, NT, NE])
        TOP = sb("TOP", [P, NT, NE])
        IDX = sb("IDX", [P, NT, NE], U32)
        IDF = sb("IDF", [P, NT, 2])
        WA = sb("WA", [P, NT, NE])
        WB = sb("WB", [P, NT, NE])
        SI = Xf[0:HIDP, 0:3 * GW].rearrange("p (s q) -> p s q", s=3)
        HH = Xf[0:HIDP, 3 * GW:6 * GW].rearrange("p (s q) -> p s q", s=3)
        YW = Xf[:, 6 * GW:6 * GW + 3 * NE * C].rearrange("p (s e c) -> p s e c", s=3, e=NE)

        bank = [ctx.enter_context(nc.psum_tensor(f"bank{i}", [P, 512], F32)) for i in range(8)]

        names = """s_x0 s_x1 s_wtok s_cst s_wa s_wf s_w2 s_txt s_out
            g_ready g_done c_bf c_bias c_ones w_split w_small w_rows w2_zero wvo_ready wvo_done bout_zero
            tok_done h_fm h_tp h_copied a_var a_rstd a_xn a_tp a_xT a_qk a_v a_sqr a_vc a_r a_q4 a_kk a_n2 a_rq a_q2n
            a_kv a_kvs a_q2tp a_q2T p_c p_rc p_kvs p_tp p_kvT p_kvo p_kvoS
            b_o b_h1 b_var b_rstd b_rr b_hn b_h2 b_tp b_hT b_q b_qkc b_rt b_hl b_qt b_qT b_kT
            s_done s_max s_nm s_ml s_mt s_mT st_done e_done m_done pv_done y_cp y_tp y_n
            w_tp w_yT w_o w_h w_ss w_rs w_fl w_ft w_fT w_r w_lg w_e w_wt
            m_a m_b m_s m_h m_y m_yw m_tr
            ve_chain ac_chain po_chain""".split()
        z = {n: sem(n) for n in names}

        block = ctx.enter_context(nc.Block())

        order = plan()

        def follow(stages):
            for kind, *args in order:
                if kind in stages:
                    stages[kind](*args)

        def linker(eng, chain):
            count = [0]

            def link(ins):
                count[0] += 1
                ins.then_inc(chain, 1)
                eng.wait_ge(chain, count[0])
            return link

        def bc(ap, shape):
            return ap.unsqueeze(len(ap.shape)).to_broadcast(shape)

        def tiles(n):
            return slice(GT * n, GT * n + GT)

        @block.sync
        def _(sp):
            sp.dma_start(dft_sb[:, :], dft).then_inc(z["s_wtok"], 16)
            sp.dma_start(Wt[:, :, :], w_tok).then_inc(z["s_wtok"], 16)
            for b in range(B):
                xb = x[b].rearrange("c (k h r) v -> h c k r v", h=2, r=RUN)
                for h in range(2):
                    sp.dma_start(X[64 * h:64 * h + 64, b, 0:NBLK - 1, :, :], xb[h]).then_inc((z["s_x0"], z["s_x1"])[b], 16)
                last = x[b][:, T - 1:T, :]
                for h in range(2):
                    for r in range(RUN):
                        sp.dma_start(X[64 * h:64 * h + 64, b, NBLK - 1, r:r + 1, :], last).then_inc((z["s_x0"], z["s_x1"])[b], 16)
            for n in range(NG):
                b, g = divmod(n, GROUPS)
                sp.wait_ge(z["m_tr"], GT * n + GT)
                sp.dma_start(out[b, GW * g:GW * g + GW, :].rearrange("(t p) c -> p t c", p=P), H[:, tiles(n), :]).then_inc(z["s_out"], 16)
            sp.wait_ge(z["s_out"], 16 * NG)

        @block.gpsimd
        def _(po):
            link = linker(po, z["po_chain"])
            po.memset(bias[:, 0:1], 1e-5)
            po.memset(bias[:, 1:2], 1e-6)
            po.memset(bias[:, 2:3], 0.0)
            po.memset(bias[:, 4:5], 1e-11)
            po.memset(bias[:, 3:4], LN2_20).then_inc(z["c_bias"], 1)
            link(po.memset(identb[:, :], 0.0))
            link(po.memset(maskb[:, :], 0.0))
            po.affine_select(out=identb[:, :], in_=identb[:, :], compare_op=ALU.not_equal, fill=1.0, base=0,
                             pattern=[[-1, P]], channel_multiplier=1).then_inc(z["c_bf"], 1)
            po.affine_select(out=maskb[:, :], in_=maskb[:, :], compare_op=ALU.is_ge, fill=NEG, base=0,
                             pattern=[[-1, P]], channel_multiplier=1).then_inc(z["c_bf"], 1)
            po.memset(W2[:, :, :], 0.0).then_inc(z["w2_zero"], 1)
            po.wait_ge(z["w2_zero"], 1)
            po.memset(bout[:, :], 0.0).then_inc(z["bout_zero"], 1)
            po.wait_ge(z["bout_zero"], 1)
            link(po.memset(VA[:, :, :, :], 0.0))
            po.memset(VA[:, :, :, HD:HD + 1], 1.0)
            po.memset(V1[:, :, :, C:C + 1], 1.0).then_inc(z["c_ones"], 1)
            po.wait_ge(z["c_ones"], 1)
            link(po.memset(QT[64:P, :, :].bitcast(F32), 0.0))
            link(po.memset(KT[64:P, :, :].bitcast(F32), 0.0))
            po.memset(KT[64:66, :, :].bitcast(F32), 1.0).then_inc(z["w_rows"], 1)
            po.wait_ge(z["w_rows"], 1)

            def a_sums(n):
                r = st[:, n, 21:27].rearrange("p (t two) -> p t two", two=2)
                q, k = QK2[:, n % 2, :, 0, :], QK2[:, n % 2, :, 1, :]
                po.wait_ge(z["a_sqr"], n + 1)
                po.tensor_tensor(Q4[:, n % 2, :, :], q, q, ALU.mult).then_inc(z["a_q4"], 1)
                po.wait_ge(z["a_r"], n + 1)
                if n >= 2:
                    po.wait_ge(z["a_kv"], n - 1)
                link(po.tensor_tensor(KK[:, n % 2, :, 0, :], k, bc(r[:, :, 1], [P, GT, C]), ALU.mult))
                po.tensor_tensor(KK[:, n % 2, :, 1, :], KK[:, n % 2, :, 0, :], KK[:, n % 2, :, 0, :], ALU.mult).then_inc(z["a_kk"], 1)

            def b_rope(n):
                g = n % GROUPS
                s = n % 2
                shape = [P, GT, 6, HD // 2]
                cb = cos[:, GT * g:GT * g + GT, :].unsqueeze(2).to_broadcast([P, GT, 6, HD])
                sn = sin[:, GT * g:GT * g + GT, :].unsqueeze(2)
                po.wait_ge(z["b_qkc"], 2 * n + 2)
                if n >= 2:
                    po.wait_ge(z["b_hl"], n - 1)
                po.tensor_tensor(RT[:, s, 0], QKs[:, s], cb, ALU.mult)
                po.tensor_tensor(RT[:, s, 1, :, :, 0:8], QKs[:, s, :, :, 8:16], sn[:, :, :, 0:8].to_broadcast(shape), ALU.mult)
                link(po.tensor_tensor(RT[:, s, 1, :, :, 8:16], QKs[:, s, :, :, 0:8], sn[:, :, :, 8:16].to_broadcast(shape), ALU.mult))
                po.tensor_tensor(RT[:, s, 0], RT[:, s, 0], RT[:, s, 1], ALU.add).then_inc(z["b_rt"], 1)

            def max_split(t, i):
                if i < len(s1_units(t)) - 1:
                    return
                po.wait_ge(z["s_nm"], t + 1)
                link(po.tensor_copy(ML[:, t, :, 0], NM[:, t, :]))
                po.tensor_tensor(ML[:, t, :, 1], NM[:, t, :], ML[:, t, :, 0], ALU.subtract).then_inc(z["s_ml"], 1)

            steps = [0]

            def causal(n, j, h):
                if h < NH - 1:
                    return
                steps[0] += 1
                if j >= GT * (n % GROUPS):
                    q0 = P * (j - GT * (n % GROUPS))
                    po.wait_ge(z["e_done"], NH * steps[0])
                    dia = PR[:, (steps[0] - 1) % PRING, :, q0:q0 + P]
                    po.affine_select(out=dia, in_=dia, compare_op=ALU.is_ge, fill=0.0, base=0,
                                     pattern=[[0, NH], [1, P]], channel_multiplier=-1).then_inc(z["m_done"], 1)

            def w_norm(n):
                po.wait_ge(z["w_ss"], n + 1)
                po.tensor_tensor(H[:, tiles(n), :], H[:, tiles(n), :], D[:, tiles(n), :], ALU.add).then_inc(z["w_h"], 1)

            follow({"a_sums": a_sums, "b_rope": b_rope, "max": max_split, "score": causal, "w_norm": w_norm})

            for n in range(NG):
                for r in range(GT):
                    t = GT * n + r
                    y = YW[:, t % 3]
                    po.wait_ge(z["m_yw"], t + 1)
                    link(po.tensor_tensor(y[:, 0:4, :], y[:, 0:4, :], y[:, 4:8, :], ALU.add))
                    link(po.tensor_tensor(y[:, 0:2, :], y[:, 0:2, :], y[:, 2:4, :], ALU.add))
                    link(po.tensor_tensor(y[:, 0, :], y[:, 0, :], y[:, 1, :], ALU.add))
                    ins = po.tensor_tensor(H[:, t, :], H[:, t, :], y[:, 0, :], ALU.add)
                    ins.then_inc(z["m_tr"], 1)

        @block.scalar
        def _(ac):
            link = linker(ac, z["ac_chain"])
            ac.dma_start(cst[:, :], consts).then_inc(z["s_cst"], 16)
            ac.dma_start(Wqkv[0:C, :], qkv_w).then_inc(z["s_wa"], 16)
            ac.dma_start(Wqkv[C:C + 1, :], qkv_b).then_inc(z["s_wa"], 16)
            ac.dma_start(WvT[:, :], w_vT).then_inc(z["s_wa"], 16)
            ac.dma_start(Wout[:, :], out_w).then_inc(z["s_wa"], 16)
            ac.dma_start(Wffn[:, :], w_ffn).then_inc(z["s_wa"], 16)
            ac.dma_start(WoT[:, :], woT).then_inc(z["s_wa"], 16)
            ac.dma_start(ln1_sb[:, :], ln1).then_inc(z["s_wa"], 16)
            ac.wait_ge(z["bout_zero"], 1)
            ac.dma_start(bout[C:C + 1, :], out_b).then_inc(z["s_wa"], 16)
            for b in range(B):
                ac.dma_start(H[:, TILES * (b + 1) - 1, :], txt[b]).then_inc(z["s_txt"], 16)
            for h in range(2):
                rows = slice(64 * h, 64 * h + 64)
                ac.dma_start(ln2_sb[rows, :], ln2).then_inc(z["s_wf"], 16)
                ac.dma_start(WR[rows, 0:NCH], w1T).then_inc(z["s_wf"], 16)
                ac.dma_start(WR[rows, NCH:2 * NCH], w3T).then_inc(z["s_wf"], 16)
                ac.dma_start(WR[rows, 2 * NCH:WCOLS], routerT).then_inc(z["s_wf"], 16)
            ac.wait_ge(z["w2_zero"], 1)
            w2v = w2T.rearrange("(q two) h c -> two h q c", two=2)
            W2v = W2[:, :, :].rearrange("h (q k) c -> h k q c", k=3)
            a, m = CUT[1], HID - CUT[1]
            ac.dma_start(W2v[0:a, 0, :, 0:C], w2v[0, 0:a]).then_inc(z["s_w2"], 16)
            ac.dma_start(W2v[0:m, 1, :, 0:C], w2v[0, a:HID]).then_inc(z["s_w2"], 16)
            ac.dma_start(W2v[m:2 * m, 1, :, C:P], w2v[1, 0:m]).then_inc(z["s_w2"], 16)
            ac.dma_start(W2v[0:a, 2, :, C:P], w2v[1, m:HID]).then_inc(z["s_w2"], 16)
            ac.wait_ge(z["c_bias"], 1)
            ac.preload_act_table_set("natural_log_exp_and_others")

            def rsqrt(dst, src, tmp, scale, eps):
                link(ac.activation(tmp, src, ACT.Ln, bias=eps, scale=scale))
                return ac.activation(dst, tmp, ACT.Exp, bias=b_zero, scale=-0.5)

            def rsqrt_tiny(dst, src, tmp, rows=P):
                link(ac.activation(tmp, src, ACT.Ln, bias=b_zero[0:rows], scale=LN_SCALE))
                return ac.activation(dst, tmp, ACT.Exp, bias=b_20[0:rows], scale=-0.5)

            def tokens(b):
                ac.wait_ge(z["tok_done"], b + 1)
                for half in range(2):
                    rows = slice(C * half, C * half + C)
                    ac.activation(hfm[rows, :].rearrange("p (v k) -> p v k", k=NPATCH),
                                  bank[6][rows, :].rearrange("p (k v) -> p v k", k=NPATCH), ACT.Copy).then_inc(z["h_fm"], 1)
                ac.wait_ge(z["h_tp"], b + 1)
                ac.activation(H[:, TILES * b:TILES * b + 8, :].rearrange("p (h t) c -> p h t c", h=2),
                              bank[7][:, :].rearrange("p (t h c) -> p h t c", t=4, h=2), ACT.Copy).then_inc(z["h_copied"], 1)

            def a_stats(n):
                ac.wait_ge(z["a_var"], n + 1)
                rsqrt(st[:, n, 12:15], MV[:, n, :, 1], st[:, n, 9:12], 1.0, b_eps5).then_inc(z["a_rstd"], 1)

            def a_norm(n):
                ac.wait_ge(z["a_tp"], n + 1)
                ac.activation(xnT[0:C, n, :], bank[6][0:C, 0:GW], ACT.Copy).then_inc(z["a_xT"], 1)

            def a_qkv(n):
                if n == 0:
                    ac.wait_ge(z["c_ones"], 1)
                    ac.wait_ge(z["w_split"], 1)
                if n >= 2:
                    ac.wait_ge(z["a_q2n"], n - 1)
                    ac.wait_ge(z["a_kv"], n - 1)
                ac.wait_ge(z["a_qk"], n + 1)
                ac.activation(QK2[:, n % 2, :, :, :].rearrange("p t a c -> p (t a c)"), bank[7][:, 0:GT * P], ACT.Square).then_inc(z["a_sqr"], 1)
                ac.wait_ge(z["a_v"], n + 1)
                ac.activation(V1[:, n % 2, :, 0:C], bank[6][:, 0:GT * C].rearrange("p (t c) -> p t c", c=C), ACT.Copy).then_inc(z["a_vc"], 1)

            def a_sums(n):
                ac.wait_ge(z["a_n2"], n + 1)
                rsqrt_tiny(st[:, n, 33:36], st[:, n, 27:30], st[:, n, 30:33]).then_inc(z["a_rq"], 1)

            def a_kv(n):
                ac.wait_ge(z["a_q2tp"], n + 1)
                ac.activation(q2T[:, n, :], bank[6][0:C, 0:GW], ACT.Copy).then_inc(z["a_q2T"], 1)

            def kv(b):
                ac.wait_ge(z["p_c"], b + 1)
                rsqrt_tiny(kst[:, b, 2:3], kst[:, b, 0:1], kst[:, b, 1:2], C).then_inc(z["p_rc"], 1)

            def b_out(n):
                ac.wait_ge(z["b_var"], n + 1)
                rsqrt(st[:, n, 18:21], MV[:, n, :, 1], st[:, n, 15:18], 1 + 1e-6, b_eps11).then_inc(z["b_rr"], 1)
                rsqrt(st[:, n, 12:15], MV[:, n, :, 1], st[:, n, 9:12], 1.0, b_eps5).then_inc(z["b_rstd"], 1)

            def b_turn(n):
                ac.wait_ge(z["b_tp"], n + 1)
                ac.activation(hnT[:, n % 2, :], bank[6][0:C, 0:GW], ACT.Copy).then_inc(z["b_hT"], 1)

            def b_qkv(n):
                ac.wait_ge(z["b_q"], n + 1)
                if n >= 2:
                    ac.wait_ge(z["b_rt"], n - 1)
                q = bank[7][:, 0:GT * P].rearrange("p (t c) -> p t c", c=P)
                ac.activation(QKs[:, n % 2, :, :, :].rearrange("p t h e -> p t (h e)"), q[:, :, 0:96], ACT.Copy).then_inc(z["b_qkc"], 1)
                ac.activation(VA[:, tiles(n), :, 0:HD], q[:, :, 96:128].rearrange("p t (v e) -> p t v e", e=HD), ACT.Copy).then_inc(z["b_qkc"], 1)

            def b_qk(n):
                for t in range(GT * n, GT * n + GT):
                    ac.wait_ge(z["b_qt"], t + 1)
                    ac.activation(QT[0:64, :, t * P:t * P + P], bank[6][0:64, :].rearrange("p (h q) -> p h q", h=NH), ACT.Copy).then_inc(z["b_qT"], 1)

            units = [0]

            def score(n, j, h):
                q0 = max(0, P * (j - GT * (n % GROUPS)))
                u = units[0]
                units[0] += 1
                step = u // NH
                if step >= PRING and h == 0:
                    ac.wait_ge(z["pv_done"], step - PRING + 1)
                ac.wait_ge(z["st_done"], u + 1)
                ac.activation(PR[:, step % PRING, h, q0:GW], bank[2 + u % 3][:, q0:GW], ACT.Exp,
                              bias=b_zero, scale=HD ** -0.5).then_inc(z["e_done"], 1)

            def y_copy(n):
                ac.wait_ge(z["pv_done"], units[0] // NH)
                if n >= 2:
                    ac.wait_ge(z["y_tp"], n - 1)
                ac.activation(YS[:, n % 2, :], bank[5][:, 0:GW], ACT.Copy).then_inc(z["y_cp"], 1)

            def w_turn(n):
                ac.wait_ge(z["w_tp"], n + 1)
                ac.activation(yT[:, n % 2, :], bank[6][0:C, 0:GW], ACT.Copy).then_inc(z["w_yT"], 1)

            def w_out(n):
                ac.wait_ge(z["w_ss"], n + 1)
                rsqrt(st[:, n, 33:36], st[:, n, 27:30], st[:, n, 30:33], 1 / C, b_eps6).then_inc(z["w_rs"], 1)

            def w_split(n):
                ac.wait_ge(z["w_ft"], n + 1)
                ac.activation(FT[:, n, :], bank[6][:, 0:GW], ACT.Copy).then_inc(z["w_fT"], 1)

            def w_route(n):
                ac.wait_ge(z["w_lg"], n + 1)
                ac.activation(RL[:, tiles(n), :], RL[:, tiles(n), :], ACT.Exp, bias=b_zero).then_inc(z["w_e"], 1)

            follow({"tokens": tokens, "a_stats": a_stats, "a_norm": a_norm, "a_qkv": a_qkv, "a_sums": a_sums, "a_kv": a_kv,
                    "kv": kv, "b_out": b_out, "b_turn": b_turn, "b_qkv": b_qkv, "b_qk": b_qk, "score": score,
                    "y_copy": y_copy, "w_turn": w_turn, "w_out": w_out, "w_split": w_split, "w_route": w_route})

            u = 0
            for n in range(NG):
                for c in range(CHUNKS):
                    m = chunk(c)[1]
                    ac.wait_ge(z["m_a"], u + 1)
                    if u >= 3:
                        ac.wait_ge(z["m_h"], u - 2)
                    ac.activation(SI[0:m, u % 3, :], bank[u % 2][0:m, 0:GW], ACT.Silu, bias=b_zero[0:m]).then_inc(z["m_s"], 1)
                    u += 1

        @block.vector
        def _(ve):
            link = linker(ve, z["ve_chain"])
            ve.wait_ge(z["g_ready"], 1)
            for h in range(2):
                for a in range(2):
                    src = bank[2 + a][64 * h:64 * h + 64, :].rearrange("p (o j h r) -> p h j r o", o=32, j=2, h=2)[:, h]
                    ins = ve.tensor_copy(G[64 * h:64 * h + 64, :, :, 32 * a:32 * a + 32], src)
            ins.then_inc(z["g_done"], 1)
            ve.memset(xnT[C:C + 1, :, :], 1.0)
            ve.wait_ge(z["s_wa"], 16 * 8)
            qk = Wqkv[:, 0:P].rearrange("p (a c) -> p a c", a=2)
            link(ve.tensor_reduce(wmean[:, :], qk, AX.X, ALU.add))
            link(ve.tensor_scalar(wmean[:, :], wmean[:, :], -1 / C, None, ALU.mult))
            ve.tensor_tensor(qk, qk, bc(wmean[:, :], [C + 1, 2, C]), ALU.add)
            ve.tensor_scalar(Wffn[:, :], Wffn[:, :], ln1_sb[:, 0:1], None, ALU.mult).then_inc(z["w_small"], 1)
            ve.wait_ge(z["wvo_ready"], 1)
            ve.tensor_tensor(WVO[:, :], bank[6][0:C + 1, P:P + C], bout[:, :], ALU.add).then_inc(z["wvo_done"], 1)
            ve.wait_ge(z["s_wf"], 16 * 8)
            link(ve.tensor_scalar(WR[:, :], WR[:, :], ln2_sb[:, 0:1], None, ALU.mult))
            link(ve.tensor_copy(WH[:, :], WR[:, :]))
            ve.tensor_tensor(WL[:, :], WR[:, :], WH[:, :], ALU.subtract).then_inc(z["w_split"], 1)

            def stats(n, done):
                for r in range(GT):
                    ins = ve.bn_stats(BN[:, n, r, :], H[:, GT * n + r, :])
                link(ins)
                for r in range(GT):
                    ins = ve.bn_aggr(MV[:, n, r, :], BN[:, n, r, :])
                ins.then_inc(done, 1)

            def normalised(n, dst, rstd, done):
                for r in range(GT):
                    ins = ve.tensor_scalar(dst(r), H[:, GT * n + r, :], MV[:, n, r, 0:1], st[:, n, rstd + r:rstd + r + 1], ALU.subtract, ALU.mult)
                ins.then_inc(done, 1)

            def a_stats(n):
                ve.wait_ge(z["h_copied"], n // GROUPS + 1)
                if n % GROUPS == GROUPS - 1:
                    ve.wait_ge(z["s_txt"], 16 * B)
                stats(n, z["a_var"])

            def a_norm(n):
                ve.wait_ge(z["a_rstd"], n + 1)
                normalised(n, lambda r: D[:, GT * n + r, :], 12, z["a_xn"])

            def a_sums(n):
                r = st[:, n, 21:27]
                ve.wait_ge(z["a_sqr"], n + 1)
                link(ve.tensor_reduce(st[:, n, 15:21], QK2[:, n % 2, :, :, :].rearrange("p t a c -> p (t a) c"), AX.X, ALU.add))
                link(ve.tensor_scalar(r, st[:, n, 15:21], 1e-7, None, ALU.add))
                ve.reciprocal(r, r).then_inc(z["a_r"], 1)
                ve.wait_ge(z["a_r"], n + 1)
                rq = r.rearrange("p (t two) -> p t two", two=2)[:, :, 0]
                ve.wait_ge(z["a_q4"], n + 1)
                link(ve.tensor_reduce(st[:, n, 27:30], Q4[:, n % 2, :, :], AX.X, ALU.add))
                link(ve.tensor_tensor(st[:, n, 27:30], st[:, n, 27:30], rq, ALU.mult))
                link(ve.tensor_tensor(st[:, n, 27:30], st[:, n, 27:30], rq, ALU.mult))
                ve.tensor_scalar(st[:, n, 27:30], st[:, n, 27:30], 1e-24, None, ALU.max).then_inc(z["a_n2"], 1)

            def a_kv(n):
                b, g = divmod(n, GROUPS)
                rq = st[:, n, 21:27].rearrange("p (t two) -> p t two", two=2)[:, :, 0]
                ve.wait_ge(z["a_rq"], n + 1)
                link(ve.tensor_tensor(st[:, n, 36:39], st[:, n, 33:36], rq, ALU.mult))
                if n >= 2:
                    ve.wait_ge(z["a_q2tp"], n - 1)
                for r in range(GT):
                    ins = ve.tensor_scalar(Q2[:, n % 2, r, :], QK2[:, n % 2, r, 0, :], st[:, n, 36 + r:37 + r], None, ALU.mult)
                ins.then_inc(z["a_q2n"], 1)
                ve.wait_ge(z["a_kv"], n + 1)
                if g == 0:
                    ins = ve.tensor_copy(KVA[:, b, :], bank[7][:, 0:C + 1])
                else:
                    ve.wait_ge(z["a_kvs"], n)
                    ins = ve.tensor_tensor(KVA[:, b, :], KVA[:, b, :], bank[7][:, 0:C + 1], ALU.add)
                ins.then_inc(z["a_kvs"], 1)

            def kv(b):
                ve.wait_ge(z["a_kvs"], GROUPS * (b + 1))
                ve.tensor_scalar(kst[:, b, 0:1], KVA[C:P, b, C:C + 1], 1e-24, None, ALU.max).then_inc(z["p_c"], 1)
                ve.wait_ge(z["p_rc"], b + 1)
                ve.tensor_scalar(KVS[:, b, :], KVA[0:C, b, 0:C], kst[:, b, 2:3], L ** -0.5, ALU.mult, ALU.mult).then_inc(z["p_kvs"], 1)
                ve.wait_ge(z["p_tp"], b + 1)
                ve.tensor_copy(KVST[:, b, :], bank[6][0:C, 0:C]).then_inc(z["p_kvT"], 1)
                ve.wait_ge(z["p_kvo"], b + 1)
                ve.tensor_copy(KVO[:, b, :], bank[7][0:C, 0:C]).then_inc(z["p_kvoS"], 1)

            def b_out(n):
                ve.wait_ge(z["b_o"], n + 1)
                ve.tensor_tensor(H[:, tiles(n), :], H[:, tiles(n), :], bank[7][:, 0:GT * C].rearrange("p (t c) -> p t c", c=C), ALU.add).then_inc(z["b_h1"], 1)
                ve.wait_ge(z["b_h1"], n + 1)
                stats(n, z["b_var"])

            def b_norm(n):
                ve.wait_ge(z["b_rr"], n + 1)
                if n >= 2:
                    ve.wait_ge(z["b_tp"], n - 1)
                normalised(n, lambda r: HN[:, n % 2, r, :], 18, z["b_hn"])
                ve.wait_ge(z["b_rstd"], n + 1)
                normalised(n, lambda r: D[:, GT * n + r, :], 12, z["b_h2"])

            def b_split(n):
                s = n % 2
                ve.wait_ge(z["b_rt"], n + 1)
                if n >= 2:
                    ve.wait_ge(z["b_qt"], GT * (n - 1))
                link(ve.tensor_copy(HL[:, s, :, :, 0, :], RT[:, s, 0]))
                link(ve.tensor_tensor(HL[:, s, :, :, 1, :], RT[:, s, 0], HL[:, s, :, :, 0, :], ALU.subtract))
                for slot in range(2):
                    ve.tensor_copy(HL[:, s, :, 0:NH, 2 + slot, :], HL[:, s, :, 0:NH, 1 - slot, :])
                ve.tensor_copy(HL[:, s, :, NH:6, 2:4, :].rearrange("p t h a e -> p t h (a e)"),
                               HL[:, s, :, NH:6, 0:2, :].rearrange("p t h a e -> p t h (a e)")).then_inc(z["b_hl"], 1)

            def b_qk(n):
                for t in range(GT * n, GT * n + GT):
                    ve.wait_ge(z["b_qt"], t + 1)
                    ve.tensor_copy(KT[0:64, :, t * P:t * P + P], bank[7][0:64, 0:NKV * P].rearrange("p (h q) -> p h q", h=NKV)).then_inc(z["b_kT"], 1)

            unit = [0]

            def row_max(t, i):
                h, k, w, _ = s1_units(t)[i]
                u = unit[0]
                unit[0] += 1
                ve.wait_ge(z["s_done"], u + 1)
                ve.tensor_reduce(MXC[:, t, h, k // 512:k // 512 + 1], bank[u % 2][:, 0:w], AX.X, ALU.max, negate=True).then_inc(z["s_max"], 1)
                if i == len(s1_units(t)) - 1:
                    ve.wait_ge(z["s_max"], unit[0])
                    ve.tensor_reduce(NM[:, t, :], MXC[:, t, :, 0:s1_chunks(t)], AX.X, ALU.min).then_inc(z["s_nm"], 1)

            def max_row(t):
                ve.wait_ge(z["s_mt"], t + 1)
                ve.tensor_copy(QT[64:66, :, t * P:t * P + P], bank[6][0:2, :].rearrange("p (h q) -> p h q", h=NH)).then_inc(z["s_mT"], 1)

            def y_turn(n):
                ve.wait_ge(z["y_tp"], n + 1)
                y = bank[7][:, 0:GT * P].rearrange("p (t h e) -> p t h e", t=GT, h=NH)
                rs = st[:, n, 40:52].rearrange("p (t h) -> p t h", t=GT)
                link(ve.reciprocal(rs, y[:, :, :, HD]))
                ve.tensor_tensor(YN[:, tiles(n), :, :], y[:, :, :, 0:HD], bc(rs, [P, GT, NH, HD]), ALU.mult).then_inc(z["y_n"], 1)

            def w_out(n):
                ve.wait_ge(z["w_o"], n + 1)
                link(ve.tensor_tensor(D[:, tiles(n), :], D[:, tiles(n), :], bank[7][:, 0:GT * C].rearrange("p (t c) -> p t c", c=C), ALU.add))
                for r in range(GT):
                    x2 = D[:, GT * n + r, :]
                    ins = ve.tensor_tensor_reduce(SQ[:, n % 2, r, :], x2, x2, 1.0, 0.0, ALU.mult, ALU.add, st[:, n, 27 + r:28 + r])
                ins.then_inc(z["w_ss"], 1)

            def w_norm(n):
                ve.wait_ge(z["w_rs"], n + 1)
                ve.wait_ge(z["w_h"], n + 1)
                for r in range(GT):
                    x2 = D[:, GT * n + r, :]
                    ins = ve.tensor_scalar(x2, x2, st[:, n, 33 + r:34 + r], None, ALU.mult)
                link(ins)
                if n >= 2:
                    ve.wait_ge(z["w_ft"], n - 1)
                link(ve.tensor_copy(FL[:, n % 2, :, 0, :], D[:, tiles(n), :]))
                ve.tensor_tensor(FL[:, n % 2, :, 1, :], D[:, tiles(n), :], FL[:, n % 2, :, 0, :], ALU.subtract).then_inc(z["w_fl"], 1)

            def w_route(n):
                t3 = tiles(n)
                ve.wait_ge(z["w_r"], n + 1)
                lg = bank[7][:, 0:GT * NE].rearrange("p (t e) -> p t e", e=NE)
                link(ve.tensor_reduce(st[:, n, 52:55], lg, AX.X, ALU.max, negate=True))
                ve.tensor_tensor(RL[:, t3, :], lg, bc(st[:, n, 52:55], [P, GT, NE]), ALU.add).then_inc(z["w_lg"], 1)
                ve.wait_ge(z["w_e"], n + 1)
                ve.tensor_reduce(st[:, n, 55:58], RL[:, t3, :], AX.X, ALU.add)
                for t in range(GT * n, GT * n + GT):
                    ins = ve.max(TOP[:, t, :], RL[:, t, :])
                link(ins)
                for t in range(GT * n, GT * n + GT):
                    ins = ve.max_index(IDX[:, t, :], TOP[:, t, :], RL[:, t, :])
                link(ins)
                ve.tensor_copy(IDF[:, t3, :], IDX[:, t3, 0:2])
                link(ve.tensor_tensor(st[:, n, 58:61], TOP[:, t3, 0], TOP[:, t3, 1], ALU.add))
                link(ve.scalar_tensor_tensor(out=st[:, n, 58:61], in0=st[:, n, 55:58], scalar=1e-9, in1=st[:, n, 58:61],
                                             op0=ALU.mult, op1=ALU.add))
                link(ve.reciprocal(st[:, n, 58:61], st[:, n, 58:61]))
                for t in range(GT * n, GT * n + GT):
                    ve.tensor_scalar(WA[:, t, :], iota, IDF[:, t, 0:1], TOP[:, t, 0:1], ALU.is_equal, ALU.mult)
                    ins = ve.tensor_scalar(WB[:, t, :], iota, IDF[:, t, 1:2], TOP[:, t, 1:2], ALU.is_equal, ALU.mult)
                link(ins)
                link(ve.tensor_tensor(WA[:, t3, :], WA[:, t3, :], WB[:, t3, :], ALU.add))
                ve.tensor_tensor(WA[:, t3, :], WA[:, t3, :], bc(st[:, n, 58:61], [P, GT, NE]), ALU.mult).then_inc(z["w_wt"], 1)

            follow({"a_stats": a_stats, "a_norm": a_norm, "a_sums": a_sums, "a_kv": a_kv, "kv": kv, "b_out": b_out, "b_norm": b_norm,
                    "b_split": b_split, "b_qk": b_qk, "max": row_max, "max_row": max_row, "y_turn": y_turn,
                    "w_out": w_out, "w_norm": w_norm, "w_route": w_route})
            ve.wait_ge(z["w_wt"], NG)

            u = 0
            for n in range(NG):
                for c in range(CHUNKS):
                    m = chunk(c)[1]
                    ve.wait_ge(z["m_s"], u + 1)
                    ve.wait_ge(z["m_b"], u + 1)
                    if u >= 3:
                        ve.wait_ge(z["m_y"], u - 2)
                    ve.tensor_tensor(HH[0:m, u % 3, :], SI[0:m, u % 3, :], bank[2 + u % 2][0:m, 0:GW], ALU.mult).then_inc(z["m_h"], 1)
                    u += 1
                for r in range(GT):
                    t = GT * n + r
                    ve.wait_ge(z["m_y"], CHUNKS * (n + 1))
                    if t >= 3:
                        ve.wait_ge(z["m_tr"], t - 2)
                    ve.tensor_tensor(YW[:, t % 3], bank[4 + r][:, :].rearrange("p (e c) -> p e c", c=C), bc(WA[:, t, :], [P, NE, C]), ALU.mult).then_inc(z["m_yw"], 1)

        @block.tensor
        def _(pe):
            pe.wait_ge(z["s_wtok"], 32)
            for o in range(C):
                for h in range(2):
                    ins = pe.matmul(bank[2 + o // 32][64 * h:64 * h + 64, (o % 32) * PATCH:(o % 32 + 1) * PATCH], Wt[:, o, :], dft_sb[:, :],
                                    start=True, stop=True, tile_position=(0, 64 * h))
            ins.then_inc(z["g_ready"], 1)
            pe.wait_ge(z["s_wa"], 16 * 8)
            pe.matmul(bank[6][0:C + 1, P:P + C], WvT[:, :], Wout[:, :], start=True, stop=True).then_inc(z["wvo_ready"], 1)
            pe.wait_ge(z["wvo_done"], 1)
            pe.wait_ge(z["s_cst"], 16)
            pe.wait_ge(z["g_done"], 1)

            reader = {}

            def take(i, read, count):
                if i in reader:
                    pe.wait_ge(*reader[i])
                reader[i] = (z[read], count)
                return bank[i]

            def tokens(b):
                pe.wait_ge((z["s_x0"], z["s_x1"])[b], 16 * (2 + 2 * RUN))
                dst = take(6, "h_fm", 2 * b + 2)
                taps = [(j, q) for j in range(2) for q in range(RUN)]
                for i, (j, q) in enumerate(taps):
                    for half in range(2):
                        xs = X[:, b, j:j + NPATCH, q, V // 2 * half:V // 2 * half + V // 2]
                        ins = pe.matmul(dst[C * half:C * half + C, :], G[:, j, q, :], xs, start=(i == 0), stop=(i == 2 * RUN - 1),
                                        tile_position=(0, C * half))
                ins.then_inc(z["tok_done"], 1)
                pe.wait_ge(z["h_fm"], 2 * b + 2)
                dst = take(7, "h_copied", b + 1)
                for t in range(4):
                    ins = pe.transpose(dst[:, P * t:P * t + P], hfm[:, P * t:P * t + P], ident)
                ins.then_inc(z["h_tp"], 1)

            def turn(dst, src, done):
                for r in range(GT):
                    ins = pe.transpose(dst[0:C, P * r:P * r + P], src(r), ident)
                ins.then_inc(z[done], 1)

            def a_norm(n):
                pe.wait_ge(z["a_xn"], n + 1)
                turn(take(6, "a_xT", n + 1), lambda r: D[:, GT * n + r, :], "a_tp")

            def a_qkv(n):
                if n == 0:
                    pe.wait_ge(z["w_small"], 1)
                pe.wait_ge(z["a_xT"], n + 1)
                dst = take(7, "a_sqr", n + 1)
                for r in range(GT):
                    ins = pe.matmul(dst[:, P * r:P * r + P], xnT[:, n, P * r:P * r + P], Wqkv[:, 0:P], start=True, stop=True)
                ins.then_inc(z["a_qk"], 1)
                dst = take(6, "a_vc", n + 1)
                for r in range(GT):
                    ins = pe.matmul(dst[:, C * r:C * r + C], xnT[:, n, P * r:P * r + P], Wqkv[:, P:192], start=True, stop=True)
                ins.then_inc(z["a_v"], 1)

            def a_kv(n):
                pe.wait_ge(z["a_kk"], n + 1)
                pe.wait_ge(z["a_vc"], n + 1)
                dst = take(7, "a_kvs", n + 1)
                for r in range(GT):
                    kk = KK[:, n % 2, r, :, :].rearrange("p a c -> p (a c)")
                    ins = pe.matmul(dst[:, 0:C + 1], kk, V1[:, n % 2, r, :], start=(r == 0), stop=(r == GT - 1))
                ins.then_inc(z["a_kv"], 1)
                pe.wait_ge(z["a_q2n"], n + 1)
                turn(take(6, "a_q2T", n + 1), lambda r: Q2[:, n % 2, r, :], "a_q2tp")

            def kv(b):
                pe.wait_ge(z["p_kvs"], b + 1)
                pe.transpose(take(6, "p_kvT", b + 1)[0:C, 0:C], KVS[:, b, :], ident[0:C, 0:C]).then_inc(z["p_tp"], 1)
                pe.wait_ge(z["p_kvT"], b + 1)
                pe.matmul(take(7, "p_kvoS", b + 1)[0:C, 0:C], KVST[:, b, :], Wout[:, :], start=True, stop=True).then_inc(z["p_kvo"], 1)

            def b_out(n):
                pe.wait_ge(z["p_kvoS"], n // GROUPS + 1)
                pe.wait_ge(z["a_q2T"], n + 1)
                dst = take(7, "b_h1", n + 1)
                for r in range(GT):
                    o = dst[:, C * r:C * r + C]
                    pe.matmul(o, xnT[:, n, P * r:P * r + P], WVO[:, :], start=True, stop=False)
                    ins = pe.matmul(o, q2T[:, n, P * r:P * r + P], KVO[:, n // GROUPS, :], start=False, stop=True)
                ins.then_inc(z["b_o"], 1)

            def b_turn(n):
                pe.wait_ge(z["b_hn"], n + 1)
                turn(take(6, "b_hT", n + 1), lambda r: HN[:, n % 2, r, :], "b_tp")

            def b_qkv(n):
                pe.wait_ge(z["b_hT"], n + 1)
                dst = take(7, "b_qkc", 2 * n + 2)
                for r in range(GT):
                    ins = pe.matmul(dst[:, P * r:P * r + P], hnT[:, n % 2, P * r:P * r + P], Wffn[:, :], start=True, stop=True)
                ins.then_inc(z["b_q"], 1)

            def b_qk(n):
                pe.wait_ge(z["b_hl"], n + 1)
                for t in range(GT * n, GT * n + GT):
                    src = HL[:, n % 2, t % GT].bitcast(F32).rearrange("p h a e -> p h (a e)")
                    dst = take(6, "b_qT", t + 1)
                    for h in range(NH):
                        pe.transpose(dst[0:64, P * h:P * h + P], src[:, h], ident)
                    dst = take(7, "b_kT", t + 1)
                    for h in range(NKV):
                        ins = pe.transpose(dst[0:64, P * h:P * h + P], src[:, NH + h], ident)
                    ins.then_inc(z["b_qt"], 1)

            unit = [0]

            def row_max(t, i):
                b = t // TILES
                h, k, w, diag = s1_units(t)[i]
                u = unit[0]
                unit[0] += 1
                if u == 0:
                    pe.wait_ge(z["c_bf"], 2)
                    pe.wait_ge(z["w_rows"], 1)
                if i == 0:
                    pe.wait_ge(z["b_qT"], t + 1)
                    pe.wait_ge(z["b_kT"], t + 1)
                if u >= 2:
                    pe.wait_ge(z["s_max"], u - 1)
                o = bank[u % 2]
                k0 = b * L + k
                ins = pe.matmul(o[:, 0:w], QT[:, h, t * P:t * P + P], KT[:, h // 2, k0:k0 + w], start=True, stop=not diag)
                if diag:
                    ins = pe.matmul(o[:, w - P:w], identb[:, :], maskb[:, :], start=False, stop=True)
                ins.then_inc(z["s_done"], 1)

            def max_row(t):
                pe.wait_ge(z["s_ml"], t + 1)
                dst = take(6, "s_mT", t + 1)
                for h in range(NH):
                    ins = pe.transpose(dst[0:2, P * h:P * h + P], ML[:, t, h, :].bitcast(F32), ident)
                ins.then_inc(z["s_mt"], 1)

            units = [0]
            steps = [0]
            diagonals = [0]

            def score(n, j, h):
                g = n % GROUPS
                q0 = max(0, P * (j - GT * g))
                key = (n // GROUPS) * L + P * j
                u = units[0]
                units[0] += 1
                if j == 0 and h == 0:
                    pe.wait_ge(z["s_mT"], GT * n + GT)
                if u >= 3:
                    pe.wait_ge(z["e_done"], u - 2)
                pe.matmul(bank[2 + u % 3][:, q0:GW], KT[:, h // 2, key:key + P], QT[:, h, GW * n + q0:GW * n + GW],
                          start=True, stop=True).then_inc(z["st_done"], 1)

            def weigh(n, j):
                g = n % GROUPS
                q0 = max(0, P * (j - GT * g))
                i = steps[0]
                steps[0] += 1
                if j == 0 and n:
                    pe.wait_ge(z["y_cp"], n)
                pe.wait_ge(z["e_done"], NH * (i + 1))
                if j >= GT * g:
                    diagonals[0] += 1
                    pe.wait_ge(z["m_done"], diagonals[0])
                for h in range(NH):
                    ins = pe.matmul(bank[5][32 * h:32 * h + 32, q0:GW], VA[:, (n // GROUPS) * TILES + j, h // 2, :],
                                    PR[:, i % PRING, h, q0:GW], start=(j == 0), stop=(j == GT * g + GT - 1), tile_position=(0, 32 * h))
                ins.then_inc(z["pv_done"], 1)

            def y_turn(n):
                pe.wait_ge(z["y_cp"], n + 1)
                dst = take(7, "y_n", n + 1)
                for r in range(GT):
                    ins = pe.transpose(dst[:, P * r:P * r + P], YS[:, n % 2, P * r:P * r + P], ident)
                ins.then_inc(z["y_tp"], 1)

            def w_turn(n):
                pe.wait_ge(z["y_n"], n + 1)
                turn(take(6, "w_yT", n + 1), lambda r: YN[:, GT * n + r, :, :].rearrange("p h e -> p (h e)"), "w_tp")

            def w_out(n):
                pe.wait_ge(z["w_yT"], n + 1)
                dst = take(7, "w_ss", n + 1)
                for r in range(GT):
                    ins = pe.matmul(dst[:, C * r:C * r + C], yT[:, n % 2, P * r:P * r + P], WoT[:, :], start=True, stop=True)
                ins.then_inc(z["w_o"], 1)

            def w_split(n):
                pe.wait_ge(z["w_fl"], n + 1)
                dst = take(6, "w_fT", n + 1)
                for r in range(GT):
                    src = FL[:, n % 2, r, :, :].bitcast(F32).rearrange("p a c -> p (a c)")
                    ins = pe.transpose(dst[:, P * r:P * r + P], src, ident)
                ins.then_inc(z["w_ft"], 1)

            def w_route(n):
                if n == 0:
                    pe.wait_ge(z["w_split"], 1)
                pe.wait_ge(z["w_fT"], n + 1)
                dst = take(7, "w_lg", n + 1)
                for r in range(GT):
                    for w, first in ((WH, True), (WL, False)):
                        ins = pe.matmul(dst[:, NE * r:NE * r + NE], FT[:, n, P * r:P * r + P], w[:, 2 * NCH:WCOLS], start=first, stop=not first)
                ins.then_inc(z["w_r"], 1)

            follow({"tokens": tokens, "a_norm": a_norm, "a_qkv": a_qkv, "a_kv": a_kv, "kv": kv, "b_out": b_out, "b_turn": b_turn,
                    "b_qkv": b_qkv, "b_qk": b_qk, "max": row_max, "max_row": max_row, "score": score, "weigh": weigh, "y_turn": y_turn,
                    "w_turn": w_turn, "w_out": w_out, "w_split": w_split, "w_route": w_route})

            pe.wait_ge(z["s_w2"], 64)
            pe.wait_ge(z["w_lg"], NG)

            def hidden(n, c, u):
                c0, m = chunk(c)
                for k, (base, dst, sem_) in enumerate(((0, bank[u % 2], z["m_a"]), (NCH, bank[2 + u % 2], z["m_b"]))):
                    if u >= 2:
                        pe.wait_ge((z["m_s"], z["m_h"])[k], u - 1)
                    for w, first in ((WH, True), (WL, False)):
                        ins = pe.matmul(dst[0:m, 0:GW], w[:, base + c0:base + c0 + m], FT[:, n, :], start=first, stop=not first)
                    ins.then_inc(sem_, 1)

            def combine(n, c, u):
                m = chunk(c)[1]
                pair, k = divmod(c, 3)
                lo, hi = ((0, C), (0, P), (C, P))[k]
                pe.wait_ge(z["m_h"], u + 1)
                if c == 0 and n:
                    pe.wait_ge(z["m_yw"], GT * n)
                for r in range(GT):
                    ins = pe.matmul(bank[4 + r][:, P * pair + lo:P * pair + hi], HH[0:m, u % 3, P * r:P * r + P], W2[0:m, c, lo:hi],
                                    start=(c == 0), stop=(c == CHUNKS - 1), skip_group_check=True)
                ins.then_inc(z["m_y"], 1)

            todo = [(n, c, CHUNKS * n + c) for n in range(NG) for c in range(CHUNKS)]
            for i, item in enumerate(todo):
                hidden(*item)
                if i:
                    combine(*todo[i - 1])
            combine(*todo[-1])


def kernel(x, txt, L0_tok_W, L0_attn_W_qkv, L0_attn_b_qkv, L0_attn_W_out, L0_attn_b_out, L0_ffn_ln1_w, L0_ffn_ln2_w,
           L0_ffn_wq, L0_ffn_wk, L0_ffn_wv, L0_ffn_wo, L0_ffn_router_w, L0_ffn_w1, L0_ffn_w2, L0_ffn_w3):
    import numpy as np
    import concourse.bacc as bacc
    from concourse.bass_utils import run_bass_kernel_spmd

    c = np.ascontiguousarray
    f = np.arange(PATCH // 2 + 1)[:, None] * np.arange(PATCH)[None, :] * (2 * np.pi / PATCH)
    dft = np.concatenate([np.cos(f), -np.sin(f)]) / np.sqrt(PATCH)
    inv = 1.0 / 10000.0 ** (np.arange(0, HD, 2, dtype=np.float32) / HD)
    angle = np.outer(np.arange(L, dtype=np.float32), inv)
    table = lambda a, b: np.concatenate([a, b], axis=1).reshape(TILES, P, HD).transpose(1, 0, 2).reshape(P, TILES * HD)
    consts = np.concatenate([np.eye(P), table(np.cos(angle), np.cos(angle)), table(-np.sin(angle), np.sin(angle)),
                             np.tile(np.arange(NE), (P, 1))], axis=1)
    flatT = lambda w: c(w.reshape(NCH, C).T)
    arrays = {
        "x": c(x), "txt": c(txt),
        "w_tok": c(L0_tok_W.reshape(C, NF, C).transpose(1, 0, 2)),
        "qkv_w": c(L0_attn_W_qkv), "qkv_b": c(L0_attn_b_qkv.reshape(1, 3 * C)),
        "w_vT": c(np.concatenate([L0_attn_W_qkv[:, 2 * C:], L0_attn_b_qkv[None, 2 * C:]]).T),
        "out_w": c(L0_attn_W_out), "out_b": c(L0_attn_b_out.reshape(1, C)),
        "ln1": c(L0_ffn_ln1_w.reshape(C, 1)), "ln2": c(L0_ffn_ln2_w.reshape(C, 1)),
        "w_ffn": c(np.concatenate([L0_ffn_wq, L0_ffn_wk, L0_ffn_wv]).T),
        "woT": c(L0_ffn_wo.T), "routerT": c(L0_ffn_router_w.T),
        "w1T": flatT(L0_ffn_w1), "w3T": flatT(L0_ffn_w3), "w2T": c(L0_ffn_w2.transpose(0, 2, 1)),
        "dft": dft.astype(np.float32), "consts": consts.astype(np.float32),
    }
    nc = bacc.Bacc("TRN2", target_bir_lowering=False, num_devices=1)
    args = {n: nc.dram_tensor(f"in_{n}", a.shape, F32, kind="ExternalInput").ap() for n, a in arrays.items()}
    out = nc.dram_tensor("out_h", [B, L, C], F32, kind="ExternalOutput").ap()
    build(nc, out=out, **args)
    r = run_bass_kernel_spmd(nc, [{f"in_{n}": a for n, a in arrays.items()}], core_ids=[0])
    return r.results[0]["out_h"]
```

```python
from contextlib import ExitStack

import concourse.bass as bass
from concourse import mybir

F32 = mybir.dt.float32
F32R = mybir.dt.float32r
BF16 = mybir.dt.bfloat16
U32 = mybir.dt.uint32
ALU = mybir.AluOpType
ACT = mybir.ActivationFunctionType
AX = mybir.AxisListType

P = 128
B, C, T, V = 2, 64, 128, 64
PATCH, STRIDE = 16, 8
NBLK = T // STRIDE + 1
NPATCH = T // STRIDE
NF = 2 * (PATCH // 2 + 1)
RUN = 4
TOK = V * NPATCH
TXT = 128
L = TOK + TXT
TILES = L // P
GT = 3
GROUPS = TILES // GT
NG = B * GROUPS
NT = B * TILES
GW = GT * P
NH, NKV, HD = 4, 2, 16
NE, HID = 8, 170
NCH = NE * HID
PAIRS = NE // 2
CUT = (0, 114, 226, 340)
CHUNKS = PAIRS * 3
HIDP = 114
WCOLS = 2 * NCH + NE
LN_SCALE = 2.0 ** 40
LN2_20 = 20 * 0.6931471805599453
NEG = -1e30
PRING = 4
HRING = 4
YRING = 3
MLAG = 3
FOLD = P // NF
FOLDS = -(-C // FOLD)
SPLITS = 4


def chunk(c):
    return (c // 3) * 2 * HID + CUT[c % 3], CUT[c % 3 + 1] - CUT[c % 3]


def s1_units(tile):
    n = (tile % TILES + 1) * P
    return [(h, k, min(512, n - k), k + 512 >= n) for k in range(0, n, 512) for h in range(NH)]


def s1_chunks(tile):
    return -(-(tile % TILES + 1) * P // 512)


PLAN = {
    "tokens": [(-7.71, 12.29), (13.38, 30.49)],
    "a": [(20.6, 42.03), (40, 80)],
    "b": [(47.07, 81.65), (99.22, 169.22)],
    "split": [(41.47, 71.47)],
    "max": [(84, 95), (92.66, 108), (108, 135.78), (130.97, 161.92), (165.13, 207.71), (205.27, 230.27)],
    "attend": [(101.42, 108), (108, 143.93), (140, 190), (190, 205.15), (204.41, 226.71), (233.91, 268.91)],
    "w": [(203, 239.44), (273.91, 293.91)],
    "experts": [(223.66, 243.34), (246.29, 270.76), (266.29, 286.29), (283.77, 312.37), (324.77, 338.46), (347.2, 360.53)],
    "weigh": 10,
    "mask": 2,
    "row": 1,
    "tanh": 36,
    "skew_a": 3,
    "skew_b": 2,
    "skew_w": 2,
}


def wave(groups, stages, skew):
    items = []
    for s in range(len(stages) + skew * (len(groups) - 1)):
        items += [(stages[s - skew * i], n) for i, n in enumerate(groups) if 0 <= s - skew * i < len(stages)]
    return items


def maxima_items(n):
    items, waiting = [], []
    for t in range(GT * n, GT * n + GT):
        for i in range(len(s1_units(t))):
            items.append(("max", t, i))
            if waiting and i in (PLAN["row"], PLAN["row"] + 1):
                items.append((STAGES_ROW[i - PLAN["row"]], waiting[0]))
        waiting = [t]
    return items + [(k, waiting[0]) for k in STAGES_ROW]


def attention_items(n):
    first, steps = GT * (n % GROUPS), GT * (n % GROUPS) + GT
    items = [(NH * j + h, ("score", n, j, h)) for j in range(steps) for h in range(NH)]
    items += [(NH * (j + 1) + PLAN["mask"] - 0.75, ("mask", n, j)) for j in range(first, steps)]
    items += [(NH * (j + 1) + PLAN["weigh"] - 0.5, ("weigh", n, j)) for j in range(steps)]
    return [item for _, item in sorted(items)] + [("y_copy", n), ("y_turn", n)]


def expert_items(b):
    items = []
    first, end = GROUPS * CHUNKS * b, GROUPS * CHUNKS * (b + 1)
    for u in range(first, end + MLAG + 1):
        if u > first and u - 1 < end:
            items.append(("gate", u - 1))
        if u < end:
            items.append(("hidden", u))
        if u > first + MLAG and (u - MLAG) % 3 == 0:
            items.append(("weight", (u - MLAG) // 3 - 1))
        if first <= u - MLAG < end:
            items.append(("combine", u - MLAG))
    return items


STAGES_TOKENS = [f"tap{i}" for i in range(2 * RUN)] + ["tok_copy", "tok_turn", "tok_place"]
STAGES_A = ["a_stats", "a_rstd", "a_norm", "a_turn", "a_xT", "a_qkv", "a_square", "a_r", "a_s4", "a_rq", "a_q2", "a_kv", "a_end"]
STAGES_KV = ["kv_sum", "kv_rsqrt", "kv_scale", "kv_turn", "kv_T", "kv_out", "kv_end"]
STAGES_B = ["b_mix", "b_h1", "b_rr", "b_norm", "b_turn", "b_hT", "b_proj", "b_copy", "b_rope", "b_split"] + [
    f"b_{what}{r}" for r in range(GT) for what in ("qk", "put")]
STAGES_ROW = ["row_turn", "row_put"]
STAGES_W = ["w_turn", "w_yT", "w_out", "w_x2", "w_rs", "w_norm", "w_ft", "w_fT", "w_route", "w_top", "w_exp", "w_best", "w_index", "w_weights"]
CHAINS = {k: chain for chain in (STAGES_TOKENS, STAGES_A, STAGES_KV, STAGES_B, STAGES_W, STAGES_ROW) for k in chain}
TAKES = {"tap0": ["tok_copy"], "tok_turn": ["tok_place"], "a_turn": ["a_xT"], "a_qkv": ["a_square", "a_square"],
         "a_kv": ["a_end", "a_end"], "kv_turn": ["kv_T"], "kv_out": ["kv_end"], "b_mix": ["b_h1"], "b_turn": ["b_hT"],
         "b_proj": ["b_copy"], "b_qk0": ["b_put0", "b_put0"], "b_qk1": ["b_put1", "b_put1"], "b_qk2": ["b_put2", "b_put2"],
         "w_turn": ["w_yT"], "w_out": ["w_x2"], "w_ft": ["w_fT"], "w_route": ["w_top"],
         "row_turn": ["row_put"], "y_turn": ["y_turn"], "max": ["max"], "score": ["score"], "weigh": ["y_copy"],
         "hidden": ["hidden", "gate"], "combine": ["weight"]}
BANKS = range(8)
FREED_BY = {"a_square": "a_kv", "b_norm": "b_turn", "b_turn": "b_proj", "b_copy": "b_rope", "b_rope": "b_split", "b_split": "b_qk2",
            "w_turn": "w_out", "w_norm": "w_ft"}


def needs(item):
    kind, n = item[:2]
    found = []
    if kind in CHAINS:
        i = CHAINS[kind].index(kind)
        if i:
            found.append((CHAINS[kind][i - 1], n))
        if n:
            found.append((kind, n - 1))
    if kind in FREED_BY and n >= 2:
        found.append((FREED_BY[kind], n - 2))
    if kind == "b_qk0" and n:
        found.append(("b_put2", n - 1))
    if kind == "a_stats":
        found.append(("tok_place", n // GROUPS))
    if kind == "kv_sum":
        found.append(("a_end", GROUPS * n + GROUPS - 1))
    if kind == "b_mix":
        found.append(("kv_end", n // GROUPS))
    if kind == "b_turn":
        found.append(("tok_turn", 1))
    if kind == "max" and item[2] == 0:
        found.append(("b_put2", n // GT))
    if kind == "row_turn":
        found.append(("max", n, len(s1_units(n)) - 1))
    if kind == "score" and item[2:] == (0, 0):
        found += [("row_put", GT * n + GT - 1), ("split", SPLITS)]
    if kind == "w_turn":
        found += [("y_turn", n), ("b_proj", NG - 1)]
    if kind == "hidden" and n % CHUNKS == 0:
        found += [("w_route", n // CHUNKS), ("b_mix", NG - 1)]
    if kind == "hidden" and n == PLAN["tanh"]:
        found.append(("y_turn", NG - 1))
    if kind == "weight" and n % PAIRS == 0:
        found.append(("w_weights", n // PAIRS))
    return found


def plan():
    g = [list(range(GROUPS * b, GROUPS * b + GROUPS)) for b in range(B)]
    thirds = lambda items: [items[len(items) * k // GROUPS:len(items) * (k + 1) // GROUPS] for k in range(GROUPS)]
    streams = {
        "tokens": [[(k, b) for k in STAGES_TOKENS] for b in range(B)],
        "a": [wave(g[b], STAGES_A, PLAN["skew_a"]) for b in range(B)],
        "b": [[(k, b) for k in STAGES_KV] + wave(g[b], STAGES_B, PLAN["skew_b"]) for b in range(B)],
        "split": [[("split", i) for i in range(SPLITS + 1)]],
        "max": [maxima_items(n) for n in range(NG)],
        "attend": [attention_items(n) for n in range(NG)],
        "w": [wave(g[b], STAGES_W, PLAN["skew_w"]) for b in range(B)],
        "experts": thirds(expert_items(0)) + thirds(expert_items(1)),
    }
    placed, before = [], {}
    for rank, (name, parts) in enumerate(streams.items()):
        at, previous = 0, None
        for (first, last), items in zip(PLAN[name], parts):
            for i, item in enumerate(items):
                at = max(at, first + (last - first) * (i + 0.5) / len(items))
                placed.append((at, rank, item))
                if name not in ("a", "b", "w"):
                    before[item] = previous
                previous = item
    done, order, banks = set(), [], {}
    user = {i: None for i in BANKS}
    freed = {i: 0 for i in BANKS}
    taken = {i: 0 for i in BANKS}

    def emit(item):
        if item is None or item in done:
            return
        emit(before.get(item))
        for other in needs(item):
            emit(other)
        kind, n = item[:2]
        shared = kind == "weigh" and item[2] or kind == "combine" and n % 3
        if shared:
            banks[item] = banks[item[:2] + (item[2] - 1,) if kind == "weigh" else (kind, n - 1)]
        readers = [] if shared else TAKES.get(kind, [])
        for reader in reversed(readers) if kind == "hidden" and n < PLAN["tanh"] else readers:
            if all(user.values()):
                emit(user[min(BANKS, key=lambda i: taken[i])])
            bank = min((i for i in BANKS if not user[i]), key=lambda i: freed[i])
            user[bank] = item if reader == kind else (reader, n // 3 if kind == "combine" else n)
            taken[bank] = len(order)
            banks.setdefault(item, []).append(bank)
        done.add(item)
        order.append(item)
        for i in BANKS:
            if user[i] == item:
                user[i], freed[i] = None, len(order)

    for _, _, item in sorted(placed, key=lambda x: x[:2]):
        emit(item)
    return order, banks


def build(nc, x, txt, w_tok, w_small, w_exp, w_2, dft, consts, out):
    with ExitStack() as ctx:
        def sb(name, shape, dt=F32):
            return ctx.enter_context(nc.sbuf_tensor(name, shape, dt))

        def sem(name):
            return ctx.enter_context(nc.semaphore(name))

        X = sb("X", [P, B, NBLK, RUN, V])
        early = sb("early", [P, 2 * NG * GW])
        xnT = early[0:C + 1, 0:NG * GW].rearrange("p (n q) -> p n q", n=NG)
        q2T = early[0:C, NG * GW:2 * NG * GW].rearrange("p (n q) -> p n q", n=NG)
        work = sb("work", [P, 16 * GT * C])
        Wt = work[0:FOLD * NF, 0:FOLDS * C].rearrange("p (g c) -> p g c", c=C)
        dft_sb = work[0:FOLD * NF, FOLDS * C:FOLDS * C + FOLD * PATCH]
        cut = lambda first, k, pat, **kw: work[:, first * GT * C:(first + 2 * k) * GT * C].rearrange(pat, s=2, c=C, **kw)
        SQ = cut(0, 1, "p (s t c) -> p s t c", t=GT)
        QK2 = cut(2, 2, "p (s t a c) -> p s t a c", t=GT, a=2)
        Q4 = cut(6, 1, "p (s t c) -> p s t c", t=GT)
        KK = cut(8, 2, "p (s t a c) -> p s t a c", t=GT, a=2)
        Q2 = cut(12, 1, "p (s t c) -> p s t c", t=GT)
        HN = cut(14, 1, "p (s t c) -> p s t c", t=GT)
        WH = sb("WH", [P, WCOLS], F32R)
        WL = sb("WL", [P, WCOLS], F32R)
        W2 = sb("W2", [HIDP, CHUNKS, P])
        G = sb("G", [P, 2, RUN, 64])
        cst = sb("cst", [P, 128 + 2 * TILES * HD + NE])
        ident = cst[:, 0:128]
        cos = cst[:, 128:128 + TILES * HD].rearrange("p (t e) -> p t e", e=HD)
        sin = cst[:, 128 + TILES * HD:128 + 2 * TILES * HD].rearrange("p (t e) -> p t e", e=HD)
        iota = cst[:, 128 + 2 * TILES * HD:128 + 2 * TILES * HD + NE]
        identr = sb("identr", [P, P], F32R)
        identb = sb("identb", [P, P], BF16)
        maskb = sb("maskb", [P, P], BF16)
        bias = sb("bias", [P, 5])
        b_eps5, b_eps6, b_zero, b_20, b_eps11 = (bias[:, i:i + 1] for i in range(5))
        small = sb("small", [C + 1, 578])
        Wqkv = small[:, 0:192]
        WvT, Wout, Wffn, WoT, ln1_sb = (small[0:C, a:b] for a, b in ((192, 257), (257, 321), (385, 513), (513, 577), (577, 578)))
        bout = small[:, 321:385]
        wmean = sb("wmean", [C + 1, 2])
        WVO = sb("WVO", [C + 1, C])
        KVS = sb("KVS", [C, B, C])
        KVST = sb("KVST", [C, B, C])
        KVO = sb("KVO", [C, B, C])
        st = sb("st", [P, NG, 64])
        kst = sb("kst", [C, B, 4])
        KVA = sb("KVA", [P, B, C + 1])
        BN = sb("BN", [P, NG, GT, 6])
        MV = sb("MV", [P, NG, GT, 2])
        H = sb("H", [P, NT, C])
        D = sb("D", [P, NT, C])
        V1 = sb("V1", [P, 2, GT, C + 1])
        feat = sb("feat", [P, 2, GW])
        hfm = feat[:, :, :].rearrange("p s q -> p (s q)")[:, 0:TOK // 2]
        hnT = feat[0:C, :, :]
        yT = feat[0:C, :, :]
        QKs = sb("QKs", [P, 2, GT, 6, HD])
        RT = sb("RT", [P, 2, 2, GT, 6, HD])
        HL = sb("HL", [P, 2, GT, 6, 4, HD], F32R)
        QT = sb("QT", [P, NH, NT * P], F32R)
        KT = sb("KT", [P, NKV, NT * P], F32R)
        VA = sb("VA", [P, NT, NKV, 32])
        MXC = sb("MXC", [P, NT, NH, 3])
        NM = sb("NM", [P, NT, NH])
        ML = sb("ML", [P, NT, NH, 2], F32R)
        Xf = X[:, :, :, :, :].rearrange("p b k r v -> p (b k r v)")
        WR = Xf[:, 0:WCOLS + 1]
        PR = Xf[:, 0:PRING * NH * GW].rearrange("p (s h q) -> p s h q", s=PRING, h=NH)
        yo = PRING * NH * GW
        YS = Xf[:, yo:yo + 2 * GW].rearrange("p (s q) -> p s q", s=2)
        YN = Xf[:, yo + 2 * GW:yo + 2 * GW + NT * C].rearrange("p (t h e) -> p t h e", h=NH, e=HD)
        FL = sb("FL", [P, 2, GT, 2, C], F32R)
        FT = sb("FT", [P, NG, GW], F32R)
        RL = sb("RL", [P, NT, NE])
        TOP = sb("TOP", [P, NT, NE])
        IDX = sb("IDX", [P, NT, NE], U32)
        IDF = sb("IDF", [P, NT, 2])
        WA = sb("WA", [P, NT, NE])
        WB = sb("WB", [P, NT, NE])
        SI = early[0:HIDP, 0:HRING * GW].rearrange("p (s q) -> p s q", s=HRING)
        HH = early[0:HIDP, HRING * GW:2 * HRING * GW].rearrange("p (s q) -> p s q", s=HRING)
        YW = early[:, 2 * HRING * GW:(2 * HRING + YRING) * GW].rearrange("p (s t e c) -> p s t e c", s=YRING, t=GT, e=2)

        bank = [ctx.enter_context(nc.psum_tensor(f"bank{i}", [P, 512], F32)) for i in range(8)]

        names = """s_x0 s_x1 s_wtok s_cst s_wa s_wf s_w2 s_txt s_out
            g_ready g_done c_bf c_bias c_ones w_mul w_hi w_split w_small w_ones w_rows wvo_ready wvo_done
            tok_done h_fm h_tp h_copied a_var a_rstd a_xn a_tp a_xT a_qk a_v a_sqr a_vc a_r a_q4 a_kk a_n2 a_rq a_q2n
            a_kv a_kvs a_q2tp a_q2T p_c p_rc p_kvs p_tp p_kvT p_kvo p_kvoS
            b_o b_h1 b_var b_rstd b_rr b_hn b_h2 b_tp b_hT b_q b_qkc b_rt b_hl b_qt b_qT b_kT
            s_done s_max s_nm s_ml s_mt s_mT st_done e_done m_done pv_done y_cp y_tp y_n
            w_tp w_yT w_o w_h w_ss w_rs w_fl w_ft w_fT w_r w_lg w_e w_ix w_wt
            m_a m_b m_s m_b2 m_g m_h0 m_h1 m_y m_yw m_tr
            ve_chain ac_chain po_chain""".split()
        z = {n: sem(n) for n in names}

        block = ctx.enter_context(nc.Block())

        order, banks = plan()

        def follow(stages):
            for kind, *args in order:
                if kind in stages:
                    stages[kind](*args)

        def linker(eng, chain):
            count = [0]

            def link(ins):
                count[0] += 1
                ins.then_inc(chain, 1)
                eng.wait_ge(chain, count[0])
            return link

        def gated(u):
            return (z["m_h0"], u + 1) if u < PLAN["tanh"] else (z["m_h1"], u + 1 - PLAN["tanh"])

        def bc(ap, shape):
            return ap.unsqueeze(len(ap.shape)).to_broadcast(shape)

        def tiles(n):
            return slice(GT * n, GT * n + GT)

        @block.sync
        def _(sp):
            sp.dma_start(dft_sb[:, :], dft).then_inc(z["s_wtok"], 16)
            sp.dma_start(Wt[:, :, :], w_tok).then_inc(z["s_wtok"], 16)
            for b in range(B):
                loaded = (z["s_x0"], z["s_x1"])[b]
                xb = x[b].rearrange("c (k h r) v -> h c k r v", h=2, r=RUN)
                for h in range(2):
                    rows = slice(64 * h, 64 * h + 64)
                    sp.dma_start(X[rows, b, 0:NBLK - 1, :, :], xb[h]).then_inc(loaded, 16)
                    sp.dma_start(X[rows, b, NBLK - 1, :, :], x[b][:, T - 1:T, :].to_broadcast([C, RUN, V])).then_inc(loaded, 16)
                if b == 0:
                    sp.dma_start(small[:, :], w_small).then_inc(z["s_wa"], 16)
                    sp.dma_start(cst[:, :], consts).then_inc(z["s_cst"], 16)
                    sp.dma_start(H[:, TILES - 1:NT:TILES, :], txt.rearrange("b p c -> p b c")).then_inc(z["s_txt"], 16)
            sp.wait_ge(z["tok_done"], 1)
            for h in range(2):
                sp.dma_start(WR[64 * h:64 * h + 64, :], w_exp).then_inc(z["s_wf"], 16)
            sp.dma_start(W2[:, :, :], w_2).then_inc(z["s_w2"], 16)
            for n in range(NG):
                b, g = divmod(n, GROUPS)
                sp.wait_ge(z["m_tr"], PAIRS * (n + 1))
                sp.dma_start(out[b, GW * g:GW * g + GW, :].rearrange("(t p) c -> p t c", p=P), H[:, tiles(n), :]).then_inc(z["s_out"], 16)
            sp.wait_ge(z["s_out"], 16 * NG)

        @block.gpsimd
        def _(po):
            link = linker(po, z["po_chain"])
            po.memset(bias[:, 0:1], 1e-5)
            po.memset(bias[:, 1:2], 1e-6)
            po.memset(bias[:, 2:3], 0.0)
            po.memset(bias[:, 4:5], 1e-11)
            po.memset(bias[:, 3:4], LN2_20).then_inc(z["c_bias"], 1)
            link(po.memset(identb[:, :], 0.0))
            link(po.memset(maskb[:, :], 0.0))
            po.affine_select(out=identb[:, :], in_=identb[:, :], compare_op=ALU.not_equal, fill=1.0, base=0,
                             pattern=[[-1, P]], channel_multiplier=1).then_inc(z["c_bf"], 1)
            po.affine_select(out=maskb[:, :], in_=maskb[:, :], compare_op=ALU.is_ge, fill=NEG, base=0,
                             pattern=[[-1, P]], channel_multiplier=1).then_inc(z["c_bf"], 1)
            link(po.memset(VA[:, :, :, :], 0.0))
            po.memset(VA[:, :, :, HD:HD + 1], 1.0)
            po.memset(V1[:, :, :, C:C + 1], 1.0).then_inc(z["c_ones"], 1)
            po.wait_ge(z["c_ones"], 1)
            po.memset(QT[64:P, NH // 2:, :].bitcast(F32), 0.0).then_inc(z["w_rows"], 1)
            link(po.memset(KT[64:P, :, :].bitcast(F32), 0.0))
            po.memset(KT[64:66, :, :].bitcast(F32), 1.0).then_inc(z["w_ones"], 1)
            po.wait_ge(z["w_ones"], 1)

            def split(i):
                part = lambda w, k: w[:, WCOLS // SPLITS * k:WCOLS // SPLITS * (k + 1)]
                if i == 0:
                    po.wait_ge(z["s_wf"], 32)
                if i < SPLITS:
                    po.tensor_scalar(part(WR, i), part(WR, i), WR[:, WCOLS:WCOLS + 1], None, ALU.mult).then_inc(z["w_mul"], 1)
                if i:
                    po.wait_ge(z["w_hi"], i)
                    po.tensor_tensor(part(WL, i - 1), part(WR, i - 1), part(WH, i - 1), ALU.subtract).then_inc(z["w_split"], 1)

            def a_q4(n):
                q = QK2[:, n % 2, :, 0, :]
                po.wait_ge(z["a_sqr"], n + 1)
                if n >= 2:
                    po.wait_ge(z["a_n2"], n - 1)
                po.tensor_tensor(Q4[:, n % 2, :, :], q, q, ALU.mult).then_inc(z["a_q4"], 1)

            def a_k(n):
                r = st[:, n, 21:27].rearrange("p (t two) -> p t two", two=2)
                k = QK2[:, n % 2, :, 1, :]
                po.wait_ge(z["a_r"], n + 1)
                if n >= 2:
                    po.wait_ge(z["a_kv"], n - 1)
                link(po.tensor_tensor(KK[:, n % 2, :, 0, :], k, bc(r[:, :, 1], [P, GT, C]), ALU.mult))
                po.tensor_tensor(KK[:, n % 2, :, 1, :], KK[:, n % 2, :, 0, :], KK[:, n % 2, :, 0, :], ALU.mult).then_inc(z["a_kk"], 1)

            def b_rope(n):
                g = n % GROUPS
                s = n % 2
                shape = [P, GT, 6, HD // 2]
                cb = cos[:, GT * g:GT * g + GT, :].unsqueeze(2).to_broadcast([P, GT, 6, HD])
                sn = sin[:, GT * g:GT * g + GT, :].unsqueeze(2)
                po.wait_ge(z["b_qkc"], 2 * n + 2)
                if n >= 2:
                    po.wait_ge(z["b_hl"], n - 1)
                po.tensor_tensor(RT[:, s, 0], QKs[:, s], cb, ALU.mult)
                po.tensor_tensor(RT[:, s, 1, :, :, 0:8], QKs[:, s, :, :, 8:16], sn[:, :, :, 0:8].to_broadcast(shape), ALU.mult)
                link(po.tensor_tensor(RT[:, s, 1, :, :, 8:16], QKs[:, s, :, :, 0:8], sn[:, :, :, 8:16].to_broadcast(shape), ALU.mult))
                po.tensor_tensor(RT[:, s, 0], RT[:, s, 0], RT[:, s, 1], ALU.add).then_inc(z["b_rt"], 1)

            def max_split(t, i):
                if i < len(s1_units(t)) - 1:
                    return
                po.wait_ge(z["s_nm"], t + 1)
                link(po.tensor_copy(ML[:, t, :, 0], NM[:, t, :]))
                po.tensor_tensor(ML[:, t, :, 1], NM[:, t, :], ML[:, t, :, 0], ALU.subtract).then_inc(z["s_ml"], 1)

            def mask(n, j):
                step = sum(GT * (i % GROUPS) + GT for i in range(n)) + j
                q0 = P * (j - GT * (n % GROUPS))
                po.wait_ge(z["e_done"], NH * (step + 1))
                dia = PR[:, step % PRING, :, q0:q0 + P]
                po.affine_select(out=dia, in_=dia, compare_op=ALU.is_ge, fill=0.0, base=0,
                                 pattern=[[0, NH], [1, P]], channel_multiplier=-1).then_inc(z["m_done"], 1)

            def w_norm(n):
                po.wait_ge(z["w_ss"], n + 1)
                po.tensor_tensor(H[:, tiles(n), :], H[:, tiles(n), :], D[:, tiles(n), :], ALU.add).then_inc(z["w_h"], 1)

            def w_weights(n):
                t3 = tiles(n)
                shape = [P, GT, NE]
                po.wait_ge(z["w_ix"], n + 1)
                po.tensor_tensor(WA[:, t3, :], WA[:, t3, :], bc(TOP[:, t3, 0], shape), ALU.mult)
                link(po.tensor_tensor(WB[:, t3, :], WB[:, t3, :], bc(TOP[:, t3, 1], shape), ALU.mult))
                link(po.tensor_tensor(WA[:, t3, :], WA[:, t3, :], WB[:, t3, :], ALU.add))
                po.tensor_tensor(WA[:, t3, :], WA[:, t3, :], bc(st[:, n, 58:61], shape), ALU.mult).then_inc(z["w_wt"], 1)

            def gate(u):
                if u < PLAN["tanh"]:
                    h = HH[0:chunk(u % CHUNKS)[1], u % HRING, :]
                    po.wait_ge(z["m_g"], u + 1)
                    po.wait_ge(z["m_b2"], u + 1)
                    po.tensor_tensor(h, h, SI[0:chunk(u % CHUNKS)[1], u % HRING, :], ALU.mult).then_inc(z["m_h0"], 1)

            def add(v):
                n = v // PAIRS
                if v:
                    po.wait_ge(z["m_tr"], v)
                po.wait_ge(z["m_yw"], v + 1)
                for e in range(2):
                    ins = po.tensor_tensor(H[:, tiles(n), :], H[:, tiles(n), :], YW[:, v % YRING, :, e, :], ALU.add)
                    if e == 0:
                        link(ins)
                ins.then_inc(z["m_tr"], 1)

            follow({"gate": gate, "w_weights": w_weights, "weight": add, "split": split, "a_r": a_q4, "a_s4": a_k, "b_rope": b_rope, "max": max_split, "mask": mask, "w_rs": w_norm})

        @block.scalar
        def _(ac):
            link = linker(ac, z["ac_chain"])
            ac.wait_ge(z["c_bias"], 1)
            ac.preload_act_table_set("natural_log_exp_and_others")

            def rsqrt(dst, src, tmp, scale, eps):
                link(ac.activation(tmp, src, ACT.Ln, bias=eps, scale=scale))
                return ac.activation(dst, tmp, ACT.Exp, bias=b_zero, scale=-0.5)

            def rsqrt_tiny(dst, src, tmp, rows=P):
                link(ac.activation(tmp, src, ACT.Ln, bias=b_zero[0:rows], scale=LN_SCALE))
                return ac.activation(dst, tmp, ACT.Exp, bias=b_20[0:rows], scale=-0.5)

            def split(i):
                if i < SPLITS:
                    part = lambda w: w[:, WCOLS // SPLITS * i:WCOLS // SPLITS * (i + 1)]
                    ac.wait_ge(z["w_mul"], i + 1)
                    ac.activation(part(WH), part(WR), ACT.Copy).then_inc(z["w_hi"], 1)

            def tok_copy(b):
                ac.wait_ge(z["tok_done"], b + 1)
                for half in range(2):
                    rows = slice(C * half, C * half + C)
                    ac.activation(hfm[rows, :].rearrange("p (v k) -> p v k", k=NPATCH),
                                  bank[banks["tap0", b][0]][rows, :].rearrange("p (k v) -> p v k", k=NPATCH), ACT.Copy).then_inc(z["h_fm"], 1)

            def tok_place(b):
                ac.wait_ge(z["h_tp"], b + 1)
                ac.activation(H[:, TILES * b:TILES * b + 8, :].rearrange("p (h t) c -> p h t c", h=2),
                              bank[banks["tok_turn", b][0]][:, :].rearrange("p (t h c) -> p h t c", t=4, h=2), ACT.Copy).then_inc(z["h_copied"], 1)

            def a_stats(n):
                ac.wait_ge(z["a_var"], n + 1)
                rsqrt(st[:, n, 12:15], MV[:, n, :, 1], st[:, n, 9:12], 1.0, b_eps5).then_inc(z["a_rstd"], 1)

            def a_norm(n):
                ac.wait_ge(z["a_tp"], n + 1)
                ac.activation(xnT[0:C, n, :], bank[banks["a_turn", n][0]][0:C, 0:GW], ACT.Copy).then_inc(z["a_xT"], 1)

            def a_qkv(n):
                if n == 0:
                    ac.wait_ge(z["c_ones"], 1)
                if n >= 2:
                    ac.wait_ge(z["a_q2n"], n - 1)
                    ac.wait_ge(z["a_kv"], n - 1)
                ac.wait_ge(z["a_qk"], n + 1)
                ac.activation(QK2[:, n % 2, :, :, :].rearrange("p t a c -> p (t a c)"), bank[banks["a_qkv", n][0]][:, 0:GT * P], ACT.Square).then_inc(z["a_sqr"], 1)
                ac.wait_ge(z["a_v"], n + 1)
                ac.activation(V1[:, n % 2, :, 0:C], bank[banks["a_qkv", n][1]][:, 0:GT * C].rearrange("p (t c) -> p t c", c=C), ACT.Copy).then_inc(z["a_vc"], 1)

            def a_sums(n):
                ac.wait_ge(z["a_n2"], n + 1)
                rsqrt_tiny(st[:, n, 33:36], st[:, n, 27:30], st[:, n, 30:33]).then_inc(z["a_rq"], 1)

            def a_kv(n):
                ac.wait_ge(z["a_q2tp"], n + 1)
                ac.activation(q2T[:, n, :], bank[banks["a_kv", n][1]][0:C, 0:GW], ACT.Copy).then_inc(z["a_q2T"], 1)

            def kv(b):
                ac.wait_ge(z["p_c"], b + 1)
                rsqrt_tiny(kst[:, b, 2:3], kst[:, b, 0:1], kst[:, b, 1:2], C).then_inc(z["p_rc"], 1)

            def b_out(n):
                ac.wait_ge(z["b_var"], n + 1)
                rsqrt(st[:, n, 18:21], MV[:, n, :, 1], st[:, n, 15:18], 1 + 1e-6, b_eps11).then_inc(z["b_rr"], 1)
                rsqrt(st[:, n, 12:15], MV[:, n, :, 1], st[:, n, 9:12], 1.0, b_eps5).then_inc(z["b_rstd"], 1)

            def b_turn(n):
                ac.wait_ge(z["b_tp"], n + 1)
                ac.activation(hnT[:, n % 2, :], bank[banks["b_turn", n][0]][0:C, 0:GW], ACT.Copy).then_inc(z["b_hT"], 1)

            def b_qkv(n):
                ac.wait_ge(z["b_q"], n + 1)
                if n >= 2:
                    ac.wait_ge(z["b_rt"], n - 1)
                q = bank[banks["b_proj", n][0]][:, 0:GT * P].rearrange("p (t c) -> p t c", c=P)
                ac.activation(QKs[:, n % 2, :, :, :].rearrange("p t h e -> p t (h e)"), q[:, :, 0:96], ACT.Copy).then_inc(z["b_qkc"], 1)
                ac.activation(VA[:, tiles(n), :, 0:HD], q[:, :, 96:128].rearrange("p t (v e) -> p t v e", e=HD), ACT.Copy).then_inc(z["b_qkc"], 1)

            def b_put(t):
                ac.wait_ge(z["b_qt"], t + 1)
                ac.activation(QT[0:64, :, t * P:t * P + P], bank[banks[f"b_qk{t % GT}", t // GT][0]][0:64, :].rearrange("p (h q) -> p h q", h=NH), ACT.Copy).then_inc(z["b_qT"], 1)

            units = [0]

            def score(n, j, h):
                q0 = max(0, P * (j - GT * (n % GROUPS)))
                u = units[0]
                units[0] += 1
                step = u // NH
                if step >= PRING and h == 0:
                    ac.wait_ge(z["pv_done"], step - PRING + 1)
                if u == 0:
                    ac.wait_ge(z["w_split"], SPLITS)
                ac.wait_ge(z["st_done"], u + 1)
                ac.activation(PR[:, step % PRING, h, q0:GW], bank[banks["score", n, j, h][0]][:, q0:GW], ACT.Exp,
                              bias=b_zero, scale=HD ** -0.5).then_inc(z["e_done"], 1)

            def y_copy(n):
                ac.wait_ge(z["pv_done"], units[0] // NH)
                if n >= 2:
                    ac.wait_ge(z["y_tp"], n - 1)
                ac.activation(YS[:, n % 2, :], bank[banks["weigh", n, 0][0]][:, 0:GW], ACT.Copy).then_inc(z["y_cp"], 1)

            def w_turn(n):
                ac.wait_ge(z["w_tp"], n + 1)
                ac.activation(yT[:, n % 2, :], bank[banks["w_turn", n][0]][0:C, 0:GW], ACT.Copy).then_inc(z["w_yT"], 1)

            def w_out(n):
                ac.wait_ge(z["w_ss"], n + 1)
                rsqrt(st[:, n, 33:36], st[:, n, 27:30], st[:, n, 30:33], 1 / C, b_eps6).then_inc(z["w_rs"], 1)

            def w_split(n):
                ac.wait_ge(z["w_ft"], n + 1)
                ac.activation(FT[:, n, :], bank[banks["w_ft", n][0]][:, 0:GW], ACT.Copy).then_inc(z["w_fT"], 1)

            def w_route(n):
                ac.wait_ge(z["w_lg"], n + 1)
                ac.activation(RL[:, tiles(n), :], RL[:, tiles(n), :], ACT.Exp, bias=b_zero).then_inc(z["w_e"], 1)

            def hidden(u):
                m = chunk(u % CHUNKS)[1]
                a, b = (bank[i][0:m, 0:GW] for i in banks["hidden", u])
                ac.wait_ge(z["m_a"], u + 1)
                if u >= HRING:
                    ac.wait_ge(*gated(u - HRING))
                if u >= PLAN["tanh"]:
                    ac.activation(SI[0:m, u % HRING, :], a, ACT.Silu, bias=b_zero[0:m]).then_inc(z["m_s"], 1)
                    return
                ac.activation(SI[0:m, u % HRING, :], a, ACT.Tanh, bias=b_zero[0:m], scale=0.5).then_inc(z["m_s"], 1)
                ac.wait_ge(z["m_b"], u + 1)
                if u >= HRING:
                    ac.wait_ge(z["m_y"], u - HRING + 1)
                ac.activation(HH[0:m, u % HRING, :], b, ACT.Copy, scale=0.5).then_inc(z["m_b2"], 1)

            follow({"hidden": hidden, "split": split, "tok_copy": tok_copy, "tok_place": tok_place, "a_rstd": a_stats, "a_xT": a_norm, "a_square": a_qkv, "a_rq": a_sums,
                    "a_end": a_kv, "kv_rsqrt": kv, "b_rr": b_out, "b_hT": b_turn, "b_copy": b_qkv,
                    "b_put0": lambda n: b_put(GT * n), "b_put1": lambda n: b_put(GT * n + 1), "b_put2": lambda n: b_put(GT * n + 2),
                    "score": score, "y_copy": y_copy, "w_yT": w_turn, "w_rs": w_out, "w_fT": w_split, "w_exp": w_route})

        @block.vector
        def _(ve):
            link = linker(ve, z["ve_chain"])
            ve.memset(QT[64:P, 0:NH // 2, :].bitcast(F32), 0.0).then_inc(z["w_rows"], 1)
            ve.memset(xnT[C:C + 1, :, :], 1.0)
            ve.wait_ge(z["g_ready"], 1)
            per = 4 * FOLD
            for h in range(2):
                for a in range(0, C, per):
                    k = min(per, C - a)
                    src = bank[2 + a // per][64 * h:64 * h + 64, 0:k * PATCH].rearrange("p (o j h r) -> p h j r o", o=k, j=2, h=2)[:, h]
                    ins = ve.tensor_copy(G[64 * h:64 * h + 64, :, :, a:a + k], src)
            ins.then_inc(z["g_done"], 1)
            ve.wait_ge(z["s_cst"], 16)
            ve.tensor_copy(identr[:, :], ident)
            ve.wait_ge(z["s_wa"], 16)
            qk = Wqkv[:, 0:P].rearrange("p (a c) -> p a c", a=2)
            link(ve.tensor_reduce(wmean[:, :], qk, AX.X, ALU.add))
            link(ve.tensor_scalar(wmean[:, :], wmean[:, :], -1 / C, None, ALU.mult))
            ve.tensor_tensor(qk, qk, bc(wmean[:, :], [C + 1, 2, C]), ALU.add)
            ve.tensor_scalar(Wffn[:, :], Wffn[:, :], ln1_sb[:, 0:1], None, ALU.mult).then_inc(z["w_small"], 1)
            ve.wait_ge(z["wvo_ready"], 1)
            ve.tensor_tensor(WVO[:, :], bank[6][0:C + 1, P:P + C], bout[:, :], ALU.add).then_inc(z["wvo_done"], 1)
            def stats(n, done):
                for r in range(GT):
                    ins = ve.bn_stats(BN[:, n, r, :], H[:, GT * n + r, :])
                link(ins)
                for r in range(GT):
                    ins = ve.bn_aggr(MV[:, n, r, :], BN[:, n, r, :])
                ins.then_inc(done, 1)

            def normalised(n, dst, rstd, done):
                for r in range(GT):
                    ins = ve.tensor_scalar(dst(r), H[:, GT * n + r, :], MV[:, n, r, 0:1], st[:, n, rstd + r:rstd + r + 1], ALU.subtract, ALU.mult)
                ins.then_inc(done, 1)

            def a_stats(n):
                ve.wait_ge(z["h_copied"], n // GROUPS + 1)
                if n % GROUPS == GROUPS - 1:
                    ve.wait_ge(z["s_txt"], 16)
                stats(n, z["a_var"])

            def a_norm(n):
                ve.wait_ge(z["a_rstd"], n + 1)
                normalised(n, lambda r: D[:, GT * n + r, :], 12, z["a_xn"])

            def a_r(n):
                r = st[:, n, 21:27]
                ve.wait_ge(z["a_sqr"], n + 1)
                link(ve.tensor_reduce(st[:, n, 15:21], QK2[:, n % 2, :, :, :].rearrange("p t a c -> p (t a) c"), AX.X, ALU.add))
                link(ve.tensor_scalar(r, st[:, n, 15:21], 1e-7, None, ALU.add))
                ve.reciprocal(r, r).then_inc(z["a_r"], 1)

            def a_s4(n):
                r = st[:, n, 21:27]
                ve.wait_ge(z["a_r"], n + 1)
                rq = r.rearrange("p (t two) -> p t two", two=2)[:, :, 0]
                ve.wait_ge(z["a_q4"], n + 1)
                link(ve.tensor_reduce(st[:, n, 27:30], Q4[:, n % 2, :, :], AX.X, ALU.add))
                link(ve.tensor_tensor(st[:, n, 27:30], st[:, n, 27:30], rq, ALU.mult))
                link(ve.tensor_tensor(st[:, n, 27:30], st[:, n, 27:30], rq, ALU.mult))
                ve.tensor_scalar(st[:, n, 27:30], st[:, n, 27:30], 1e-24, None, ALU.max).then_inc(z["a_n2"], 1)

            def a_q2(n):
                rq = st[:, n, 21:27].rearrange("p (t two) -> p t two", two=2)[:, :, 0]
                ve.wait_ge(z["a_rq"], n + 1)
                link(ve.tensor_tensor(st[:, n, 36:39], st[:, n, 33:36], rq, ALU.mult))
                if n >= 2:
                    ve.wait_ge(z["a_q2tp"], n - 1)
                for r in range(GT):
                    ins = ve.tensor_scalar(Q2[:, n % 2, r, :], QK2[:, n % 2, r, 0, :], st[:, n, 36 + r:37 + r], None, ALU.mult)
                ins.then_inc(z["a_q2n"], 1)

            def a_end(n):
                b, g = divmod(n, GROUPS)
                ve.wait_ge(z["a_kv"], n + 1)
                if g == 0:
                    ins = ve.tensor_copy(KVA[:, b, :], bank[banks["a_kv", n][0]][:, 0:C + 1])
                else:
                    ve.wait_ge(z["a_kvs"], n)
                    ins = ve.tensor_tensor(KVA[:, b, :], KVA[:, b, :], bank[banks["a_kv", n][0]][:, 0:C + 1], ALU.add)
                ins.then_inc(z["a_kvs"], 1)

            def kv_sum(b):
                ve.wait_ge(z["a_kvs"], GROUPS * (b + 1))
                ve.tensor_scalar(kst[:, b, 0:1], KVA[C:P, b, C:C + 1], 1e-24, None, ALU.max).then_inc(z["p_c"], 1)

            def kv_scale(b):
                ve.wait_ge(z["p_rc"], b + 1)
                ve.tensor_scalar(KVS[:, b, :], KVA[0:C, b, 0:C], kst[:, b, 2:3], L ** -0.5, ALU.mult, ALU.mult).then_inc(z["p_kvs"], 1)

            def kv_T(b):
                ve.wait_ge(z["p_tp"], b + 1)
                ve.tensor_copy(KVST[:, b, :], bank[banks["kv_turn", b][0]][0:C, 0:C]).then_inc(z["p_kvT"], 1)

            def kv_end(b):
                ve.wait_ge(z["p_kvo"], b + 1)
                ve.tensor_copy(KVO[:, b, :], bank[banks["kv_out", b][0]][0:C, 0:C]).then_inc(z["p_kvoS"], 1)

            def b_out(n):
                ve.wait_ge(z["b_o"], n + 1)
                ve.tensor_tensor(H[:, tiles(n), :], H[:, tiles(n), :], bank[banks["b_mix", n][0]][:, 0:GT * C].rearrange("p (t c) -> p t c", c=C), ALU.add).then_inc(z["b_h1"], 1)
                ve.wait_ge(z["b_h1"], n + 1)
                stats(n, z["b_var"])

            def b_norm(n):
                ve.wait_ge(z["b_rr"], n + 1)
                if n >= 2:
                    ve.wait_ge(z["b_tp"], n - 1)
                normalised(n, lambda r: HN[:, n % 2, r, :], 18, z["b_hn"])
                ve.wait_ge(z["b_rstd"], n + 1)
                normalised(n, lambda r: D[:, GT * n + r, :], 12, z["b_h2"])

            def b_split(n):
                s = n % 2
                ve.wait_ge(z["b_rt"], n + 1)
                if n >= 2:
                    ve.wait_ge(z["b_qt"], GT * (n - 1))
                link(ve.tensor_copy(HL[:, s, :, :, 0, :], RT[:, s, 0]))
                link(ve.tensor_tensor(HL[:, s, :, :, 1, :], RT[:, s, 0], HL[:, s, :, :, 0, :], ALU.subtract))
                for slot in range(2):
                    ve.tensor_copy(HL[:, s, :, 0:NH, 2 + slot, :], HL[:, s, :, 0:NH, 1 - slot, :])
                ve.tensor_copy(HL[:, s, :, NH:6, 2:4, :].rearrange("p t h a e -> p t h (a e)"),
                               HL[:, s, :, NH:6, 0:2, :].rearrange("p t h a e -> p t h (a e)")).then_inc(z["b_hl"], 1)

            def b_put(t):
                ve.wait_ge(z["b_qt"], t + 1)
                ve.tensor_copy(KT[0:64, :, t * P:t * P + P], bank[banks[f"b_qk{t % GT}", t // GT][1]][0:64, 0:NKV * P].rearrange("p (h q) -> p h q", h=NKV)).then_inc(z["b_kT"], 1)

            unit = [0]

            def row_max(t, i):
                h, k, w, _ = s1_units(t)[i]
                u = unit[0]
                unit[0] += 1
                ve.wait_ge(z["s_done"], u + 1)
                ve.tensor_reduce(MXC[:, t, h, k // 512:k // 512 + 1], bank[banks["max", t, i][0]][:, 0:w], AX.X, ALU.max, negate=True).then_inc(z["s_max"], 1)
                if i == len(s1_units(t)) - 1:
                    ve.wait_ge(z["s_max"], unit[0])
                    ve.tensor_reduce(NM[:, t, :], MXC[:, t, :, 0:s1_chunks(t)], AX.X, ALU.min).then_inc(z["s_nm"], 1)

            def row_put(t):
                ve.wait_ge(z["s_mt"], t + 1)
                ve.tensor_copy(QT[64:66, :, t * P:t * P + P], bank[banks["row_turn", t][0]][0:2, :].rearrange("p (h q) -> p h q", h=NH)).then_inc(z["s_mT"], 1)

            def y_turn(n):
                ve.wait_ge(z["y_tp"], n + 1)
                y = bank[banks["y_turn", n][0]][:, 0:GT * P].rearrange("p (t h e) -> p t h e", t=GT, h=NH)
                rs = st[:, n, 40:52].rearrange("p (t h) -> p t h", t=GT)
                link(ve.reciprocal(rs, y[:, :, :, HD]))
                ve.tensor_tensor(YN[:, tiles(n), :, :], y[:, :, :, 0:HD], bc(rs, [P, GT, NH, HD]), ALU.mult).then_inc(z["y_n"], 1)

            def w_out(n):
                ve.wait_ge(z["w_o"], n + 1)
                link(ve.tensor_tensor(D[:, tiles(n), :], D[:, tiles(n), :], bank[banks["w_out", n][0]][:, 0:GT * C].rearrange("p (t c) -> p t c", c=C), ALU.add))
                for r in range(GT):
                    x2 = D[:, GT * n + r, :]
                    ins = ve.tensor_tensor_reduce(SQ[:, n % 2, r, :], x2, x2, 1.0, 0.0, ALU.mult, ALU.add, st[:, n, 27 + r:28 + r])
                ins.then_inc(z["w_ss"], 1)

            def w_norm(n):
                ve.wait_ge(z["w_rs"], n + 1)
                ve.wait_ge(z["w_h"], n + 1)
                for r in range(GT):
                    x2 = D[:, GT * n + r, :]
                    ins = ve.tensor_scalar(x2, x2, st[:, n, 33 + r:34 + r], None, ALU.mult)
                link(ins)
                if n >= 2:
                    ve.wait_ge(z["w_ft"], n - 1)
                link(ve.tensor_copy(FL[:, n % 2, :, 0, :], D[:, tiles(n), :]))
                ve.tensor_tensor(FL[:, n % 2, :, 1, :], D[:, tiles(n), :], FL[:, n % 2, :, 0, :], ALU.subtract).then_inc(z["w_fl"], 1)

            def w_route(n):
                t3 = tiles(n)
                ve.wait_ge(z["w_r"], n + 1)
                lg = bank[banks["w_route", n][0]][:, 0:GT * NE].rearrange("p (t e) -> p t e", e=NE)
                link(ve.tensor_reduce(st[:, n, 52:55], lg, AX.X, ALU.max, negate=True))
                ve.tensor_tensor(RL[:, t3, :], lg, bc(st[:, n, 52:55], [P, GT, NE]), ALU.add).then_inc(z["w_lg"], 1)

            def w_best(n):
                t3 = tiles(n)
                ve.wait_ge(z["w_e"], n + 1)
                ve.tensor_reduce(st[:, n, 55:58], RL[:, t3, :], AX.X, ALU.add)
                for t in range(GT * n, GT * n + GT):
                    ins = ve.max(TOP[:, t, :], RL[:, t, :])
                link(ins)

            def w_index(n):
                t3 = tiles(n)
                for t in range(GT * n, GT * n + GT):
                    ins = ve.max_index(IDX[:, t, :], TOP[:, t, :], RL[:, t, :])
                link(ins)
                ve.tensor_copy(IDF[:, t3, :], IDX[:, t3, 0:2])
                link(ve.tensor_tensor(st[:, n, 58:61], TOP[:, t3, 0], TOP[:, t3, 1], ALU.add))
                link(ve.scalar_tensor_tensor(out=st[:, n, 58:61], in0=st[:, n, 55:58], scalar=1e-9, in1=st[:, n, 58:61],
                                             op0=ALU.mult, op1=ALU.add))
                shape = [P, GT, NE]
                numbers = iota.unsqueeze(1).to_broadcast(shape)
                ve.tensor_tensor(WA[:, t3, :], numbers, bc(IDF[:, t3, 0], shape), ALU.is_equal)
                ve.tensor_tensor(WB[:, t3, :], numbers, bc(IDF[:, t3, 1], shape), ALU.is_equal)
                ve.reciprocal(st[:, n, 58:61], st[:, n, 58:61]).then_inc(z["w_ix"], 1)

            def gate(u):
                m = chunk(u % CHUNKS)[1]
                ve.wait_ge(z["m_s"], u + 1)
                if u < PLAN["tanh"]:
                    si = SI[0:m, u % HRING, :]
                    ve.scalar_tensor_tensor(out=si, in0=si, scalar=1.0, in1=bank[banks["hidden", u][0]][0:m, 0:GW],
                                            op0=ALU.add, op1=ALU.mult).then_inc(z["m_g"], 1)
                    return
                ve.wait_ge(z["m_b"], u + 1)
                if u >= HRING:
                    ve.wait_ge(z["m_y"], u - HRING + 1)
                ve.tensor_tensor(HH[0:m, u % HRING, :], SI[0:m, u % HRING, :], bank[banks["hidden", u][1]][0:m, 0:GW], ALU.mult).then_inc(z["m_h1"], 1)

            def weight(v):
                n, pair = divmod(v, PAIRS)
                if pair == 0:
                    ve.wait_ge(z["w_wt"], n + 1)
                ve.wait_ge(z["m_y"], 3 * (v + 1))
                if v >= YRING:
                    ve.wait_ge(z["m_tr"], v - YRING + 1)
                y = bank[banks["combine", 3 * v][0]][:, 0:GW].rearrange("p (t e c) -> p t e c", t=GT, e=2)
                ve.tensor_tensor(YW[:, v % YRING], y, bc(WA[:, tiles(n), 2 * pair:2 * pair + 2], [P, GT, 2, C]), ALU.mult).then_inc(z["m_yw"], 1)

            follow({"gate": gate, "weight": weight, "a_stats": a_stats, "a_norm": a_norm, "a_r": a_r, "a_s4": a_s4, "a_q2": a_q2, "a_end": a_end,
                    "kv_sum": kv_sum, "kv_scale": kv_scale, "kv_T": kv_T, "kv_end": kv_end,
                    "b_h1": b_out, "b_norm": b_norm, "b_split": b_split,
                    "b_put0": lambda n: b_put(GT * n), "b_put1": lambda n: b_put(GT * n + 1), "b_put2": lambda n: b_put(GT * n + 2),
                    "max": row_max, "row_put": row_put, "y_turn": y_turn,
                    "w_x2": w_out, "w_norm": w_norm, "w_top": w_route, "w_best": w_best, "w_index": w_index})
        @block.tensor
        def _(pe):
            pe.wait_ge(z["s_wtok"], 32)
            for i in range(FOLDS):
                k = min(FOLD, C - FOLD * i)
                for h in range(2):
                    ins = pe.matmul(bank[2 + i // 4][64 * h:64 * h + 64, (i % 4) * FOLD * PATCH:((i % 4) * FOLD + k) * PATCH], Wt[0:k * NF, i, :],
                                    dft_sb[0:k * NF, 0:k * PATCH], start=True, stop=True, tile_position=(0, 64 * h))
            ins.then_inc(z["g_ready"], 1)
            pe.wait_ge(z["s_wa"], 16)
            pe.matmul(bank[6][0:C + 1, P:P + C], WvT[:, :], Wout[:, :], start=True, stop=True).then_inc(z["wvo_ready"], 1)
            pe.wait_ge(z["g_done"], 1)

            reader = {6: (z["wvo_done"], 1)}

            def take(i, read, count):
                if i in reader:
                    pe.wait_ge(*reader[i])
                reader[i] = (z[read], count)
                return bank[i]

            def tap(b, i):
                if i == 0:
                    pe.wait_ge((z["s_x0"], z["s_x1"])[b], 16 * 4)
                    take(banks["tap0", b][0], "h_fm", 2 * b + 2)
                j, q = divmod(i, RUN)
                for half in range(2):
                    xs = X[:, b, j:j + NPATCH, q, V // 2 * half:V // 2 * half + V // 2]
                    ins = pe.matmul(bank[banks["tap0", b][0]][C * half:C * half + C, :], G[:, j, q, :], xs, start=(i == 0), stop=(i == 2 * RUN - 1),
                                    tile_position=(0, C * half))
                if i == 2 * RUN - 1:
                    ins.then_inc(z["tok_done"], 1)

            def tok_turn(b):
                pe.wait_ge(z["s_cst"], 16)
                pe.wait_ge(z["h_fm"], 2 * b + 2)
                dst = take(banks["tok_turn", b][0], "h_copied", b + 1)
                for t in range(4):
                    ins = pe.transpose(dst[:, P * t:P * t + P], hfm[:, P * t:P * t + P], ident)
                ins.then_inc(z["h_tp"], 1)

            def turn(dst, src, done):
                for r in range(GT):
                    ins = pe.transpose(dst[0:C, P * r:P * r + P], src(r), ident)
                ins.then_inc(z[done], 1)

            def turn_split(dst, src):
                return pe.matmul(dst, src, identr[:, :], start=True, stop=True)

            def a_norm(n):
                pe.wait_ge(z["a_xn"], n + 1)
                turn(take(banks["a_turn", n][0], "a_xT", n + 1), lambda r: D[:, GT * n + r, :], "a_tp")

            def a_qkv(n):
                if n == 0:
                    pe.wait_ge(z["w_small"], 1)
                pe.wait_ge(z["a_xT"], n + 1)
                dst = take(banks["a_qkv", n][0], "a_sqr", n + 1)
                for r in range(GT):
                    ins = pe.matmul(dst[:, P * r:P * r + P], xnT[:, n, P * r:P * r + P], Wqkv[:, 0:P], start=True, stop=True)
                ins.then_inc(z["a_qk"], 1)
                dst = take(banks["a_qkv", n][1], "a_vc", n + 1)
                for r in range(GT):
                    ins = pe.matmul(dst[:, C * r:C * r + C], xnT[:, n, P * r:P * r + P], Wqkv[:, P:192], start=True, stop=True)
                ins.then_inc(z["a_v"], 1)

            def a_kv(n):
                pe.wait_ge(z["a_kk"], n + 1)
                pe.wait_ge(z["a_vc"], n + 1)
                dst = take(banks["a_kv", n][0], "a_kvs", n + 1)
                for r in range(GT):
                    kk = KK[:, n % 2, r, :, :].rearrange("p a c -> p (a c)")
                    ins = pe.matmul(dst[:, 0:C + 1], kk, V1[:, n % 2, r, :], start=(r == 0), stop=(r == GT - 1))
                ins.then_inc(z["a_kv"], 1)
                pe.wait_ge(z["a_q2n"], n + 1)
                turn(take(banks["a_kv", n][1], "a_q2T", n + 1), lambda r: Q2[:, n % 2, r, :], "a_q2tp")

            def kv_turn(b):
                pe.wait_ge(z["p_kvs"], b + 1)
                pe.transpose(take(banks["kv_turn", b][0], "p_kvT", b + 1)[0:C, 0:C], KVS[:, b, :], ident[0:C, 0:C]).then_inc(z["p_tp"], 1)

            def kv_out(b):
                pe.wait_ge(z["p_kvT"], b + 1)
                pe.matmul(take(banks["kv_out", b][0], "p_kvoS", b + 1)[0:C, 0:C], KVST[:, b, :], Wout[:, :], start=True, stop=True).then_inc(z["p_kvo"], 1)

            def b_out(n):
                pe.wait_ge(z["p_kvoS"], n // GROUPS + 1)
                pe.wait_ge(z["wvo_done"], 1)
                pe.wait_ge(z["a_q2T"], n + 1)
                dst = take(banks["b_mix", n][0], "b_h1", n + 1)
                for r in range(GT):
                    o = dst[:, C * r:C * r + C]
                    pe.matmul(o, xnT[:, n, P * r:P * r + P], WVO[:, :], start=True, stop=False)
                    ins = pe.matmul(o, q2T[:, n, P * r:P * r + P], KVO[:, n // GROUPS, :], start=False, stop=True)
                ins.then_inc(z["b_o"], 1)

            def b_turn(n):
                pe.wait_ge(z["b_hn"], n + 1)
                turn(take(banks["b_turn", n][0], "b_hT", n + 1), lambda r: HN[:, n % 2, r, :], "b_tp")

            def b_qkv(n):
                pe.wait_ge(z["b_hT"], n + 1)
                dst = take(banks["b_proj", n][0], "b_qkc", 2 * n + 2)
                for r in range(GT):
                    ins = pe.matmul(dst[:, P * r:P * r + P], hnT[:, n % 2, P * r:P * r + P], Wffn[:, :], start=True, stop=True)
                ins.then_inc(z["b_q"], 1)

            def b_qk(t):
                pe.wait_ge(z["b_hl"], t // GT + 1)
                src = HL[:, t // GT % 2, t % GT].rearrange("p h a e -> p h (a e)")
                dst = take(banks[f"b_qk{t % GT}", t // GT][0], "b_qT", t + 1)
                for h in range(NH):
                    turn_split(dst[0:64, P * h:P * h + P], src[:, h])
                dst = take(banks[f"b_qk{t % GT}", t // GT][1], "b_kT", t + 1)
                for h in range(NKV):
                    ins = turn_split(dst[0:64, P * h:P * h + P], src[:, NH + h])
                ins.then_inc(z["b_qt"], 1)

            unit = [0]

            def row_max(t, i):
                b = t // TILES
                h, k, w, diag = s1_units(t)[i]
                u = unit[0]
                unit[0] += 1
                if u == 0:
                    pe.wait_ge(z["c_bf"], 2)
                    pe.wait_ge(z["w_ones"], 1)
                    pe.wait_ge(z["w_rows"], 2)
                if i == 0:
                    pe.wait_ge(z["b_qT"], t + 1)
                    pe.wait_ge(z["b_kT"], t + 1)
                o = take(banks["max", t, i][0], "s_max", u + 1)
                k0 = b * L + k
                ins = pe.matmul(o[:, 0:w], QT[:, h, t * P:t * P + P], KT[:, h // 2, k0:k0 + w], start=True, stop=not diag)
                if diag:
                    ins = pe.matmul(o[:, w - P:w], identb[:, :], maskb[:, :], start=False, stop=True)
                ins.then_inc(z["s_done"], 1)

            def row_turn(t):
                pe.wait_ge(z["s_ml"], t + 1)
                dst = take(banks["row_turn", t][0], "s_mT", t + 1)
                for h in range(NH):
                    ins = turn_split(dst[0:2, P * h:P * h + P], ML[:, t, h, :])
                ins.then_inc(z["s_mt"], 1)

            units = [0]
            steps = [0]
            diagonals = [0]

            def score(n, j, h):
                g = n % GROUPS
                q0 = max(0, P * (j - GT * g))
                key = (n // GROUPS) * L + P * j
                u = units[0]
                units[0] += 1
                if j == 0 and h == 0:
                    pe.wait_ge(z["s_mT"], GT * n + GT)
                pe.matmul(take(banks["score", n, j, h][0], "e_done", u + 1)[:, q0:GW], KT[:, h // 2, key:key + P], QT[:, h, GW * n + q0:GW * n + GW],
                          start=True, stop=True).then_inc(z["st_done"], 1)

            def weigh(n, j):
                g = n % GROUPS
                q0 = max(0, P * (j - GT * g))
                i = steps[0]
                steps[0] += 1
                if j == 0:
                    take(banks["weigh", n, 0][0], "y_cp", n + 1)
                pe.wait_ge(z["e_done"], NH * (i + 1))
                if j >= GT * g:
                    diagonals[0] += 1
                    pe.wait_ge(z["m_done"], diagonals[0])
                for h in range(NH):
                    ins = pe.matmul(bank[banks["weigh", n, 0][0]][32 * h:32 * h + 32, q0:GW], VA[:, (n // GROUPS) * TILES + j, h // 2, :],
                                    PR[:, i % PRING, h, q0:GW], start=(j == 0), stop=(j == GT * g + GT - 1), tile_position=(0, 32 * h))
                ins.then_inc(z["pv_done"], 1)

            def y_turn(n):
                pe.wait_ge(z["y_cp"], n + 1)
                dst = take(banks["y_turn", n][0], "y_n", n + 1)
                for r in range(GT):
                    ins = pe.transpose(dst[:, P * r:P * r + P], YS[:, n % 2, P * r:P * r + P], ident)
                ins.then_inc(z["y_tp"], 1)

            def w_turn(n):
                pe.wait_ge(z["y_n"], n + 1)
                turn(take(banks["w_turn", n][0], "w_yT", n + 1), lambda r: YN[:, GT * n + r, :, :].rearrange("p h e -> p (h e)"), "w_tp")

            def w_out(n):
                pe.wait_ge(z["w_yT"], n + 1)
                dst = take(banks["w_out", n][0], "w_ss", n + 1)
                for r in range(GT):
                    ins = pe.matmul(dst[:, C * r:C * r + C], yT[:, n % 2, P * r:P * r + P], WoT[:, :], start=True, stop=True)
                ins.then_inc(z["w_o"], 1)

            def w_split(n):
                pe.wait_ge(z["w_fl"], n + 1)
                dst = take(banks["w_ft", n][0], "w_fT", n + 1)
                for r in range(GT):
                    ins = turn_split(dst[:, P * r:P * r + P], FL[:, n % 2, r, :, :].rearrange("p a c -> p (a c)"))
                ins.then_inc(z["w_ft"], 1)

            def w_route(n):
                if n == 0:
                    pe.wait_ge(z["w_split"], SPLITS)
                pe.wait_ge(z["w_fT"], n + 1)
                dst = take(banks["w_route", n][0], "w_lg", n + 1)
                for r in range(GT):
                    for w, first in ((WH, True), (WL, False)):
                        ins = pe.matmul(dst[:, NE * r:NE * r + NE], FT[:, n, P * r:P * r + P], w[:, 2 * NCH:WCOLS], start=first, stop=not first)
                ins.then_inc(z["w_r"], 1)

            def tap_of(i):
                return lambda b: tap(b, i)

            def hidden(u):
                n, c = divmod(u, CHUNKS)
                c0, m = chunk(c)
                k = PLAN["tanh"]
                read = (("m_g", u + 1), ("m_b2", u + 1)) if u < k else (("m_s", u + 1), ("m_h1", u + 1 - k))
                for i, base, done, by in zip(banks["hidden", u], (0, NCH), ("m_a", "m_b"), read):
                    dst = take(i, *by)
                    for w, first in ((WH, True), (WL, False)):
                        ins = pe.matmul(dst[0:m, 0:GW], w[:, base + c0:base + c0 + m], FT[:, n, :], start=first, stop=not first)
                    ins.then_inc(z[done], 1)

            def combine(u):
                n, c = divmod(u, CHUNKS)
                m = chunk(c)[1]
                v = u // 3
                lo, hi = ((0, C), (0, P), (C, P))[c % 3]
                if u == 0:
                    pe.wait_ge(z["s_w2"], 16)
                dst = take(banks["combine", u][0], "m_yw", v + 1) if c % 3 == 0 else bank[banks["combine", u][0]]
                pe.wait_ge(*gated(u))
                for r in range(GT):
                    ins = pe.matmul(dst[:, P * r + lo:P * r + hi], HH[0:m, u % HRING, P * r:P * r + P], W2[0:m, c, lo:hi],
                                    start=(c % 3 == 0 and r == 0), stop=(c % 3 == 2 and r == GT - 1), skip_group_check=True)
                ins.then_inc(z["m_y"], 1)

            stages = {f"tap{i}": tap_of(i) for i in range(2 * RUN)}
            stages.update({"hidden": hidden, "combine": combine, "tok_turn": tok_turn, "a_turn": a_norm, "a_qkv": a_qkv, "a_kv": a_kv, "kv_turn": kv_turn, "kv_out": kv_out,
                           "b_mix": b_out, "b_turn": b_turn, "b_proj": b_qkv,
                           "b_qk0": lambda n: b_qk(GT * n), "b_qk1": lambda n: b_qk(GT * n + 1), "b_qk2": lambda n: b_qk(GT * n + 2),
                           "max": row_max, "row_turn": row_turn, "score": score, "weigh": weigh, "y_turn": y_turn,
                           "w_turn": w_turn, "w_out": w_out, "w_ft": w_split, "w_route": w_route})
            follow(stages)



def kernel(x, txt, L0_tok_W, L0_attn_W_qkv, L0_attn_b_qkv, L0_attn_W_out, L0_attn_b_out, L0_ffn_ln1_w, L0_ffn_ln2_w,
           L0_ffn_wq, L0_ffn_wk, L0_ffn_wv, L0_ffn_wo, L0_ffn_router_w, L0_ffn_w1, L0_ffn_w2, L0_ffn_w3):
    import numpy as np
    import concourse.bacc as bacc
    from concourse.bass_utils import run_bass_kernel_spmd

    c = np.ascontiguousarray
    f = np.arange(PATCH // 2 + 1)[:, None] * np.arange(PATCH)[None, :] * (2 * np.pi / PATCH)
    dft = np.concatenate([np.cos(f), -np.sin(f)]) / np.sqrt(PATCH)
    inv = 1.0 / 10000.0 ** (np.arange(0, HD, 2, dtype=np.float32) / HD)
    angle = np.outer(np.arange(L, dtype=np.float32), inv)
    table = lambda a, b: np.concatenate([a, b], axis=1).reshape(TILES, P, HD).transpose(1, 0, 2).reshape(P, TILES * HD)
    consts = np.concatenate([np.eye(P), table(np.cos(angle), np.cos(angle)), table(-np.sin(angle), np.sin(angle)),
                             np.tile(np.arange(NE), (P, 1))], axis=1)
    blocks = np.zeros((FOLD * NF, FOLD * PATCH))
    for i in range(FOLD):
        blocks[NF * i:NF * (i + 1), PATCH * i:PATCH * (i + 1)] = dft
    w_tok = np.zeros((FOLDS * FOLD * NF, C), np.float32)
    w_tok[0:C * NF] = L0_tok_W.reshape(C * NF, C)
    w_tok = w_tok.reshape(FOLDS, FOLD * NF, C).transpose(1, 0, 2)
    small = np.zeros((C + 1, 578), np.float32)
    small[0:C, 0:192], small[C, 0:192] = L0_attn_W_qkv, L0_attn_b_qkv
    small[0:C, 192:256], small[0:C, 256] = L0_attn_W_qkv[:, 2 * C:].T, L0_attn_b_qkv[2 * C:]
    small[0:C, 257:321], small[C, 321:385] = L0_attn_W_out, L0_attn_b_out
    small[0:C, 385:513] = np.concatenate([L0_ffn_wq, L0_ffn_wk, L0_ffn_wv]).T
    small[0:C, 513:577], small[0:C, 577] = L0_ffn_wo.T, L0_ffn_ln1_w
    w_exp = np.concatenate([L0_ffn_w1.reshape(NCH, C).T, L0_ffn_w3.reshape(NCH, C).T, L0_ffn_router_w.T, L0_ffn_ln2_w[:, None]], axis=1)
    pairs = np.zeros((PAIRS, 2 * HID, 2, C), np.float32)
    pairs[:, 0:HID, 0] = L0_ffn_w2[0::2].transpose(0, 2, 1)
    pairs[:, HID:, 1] = L0_ffn_w2[1::2].transpose(0, 2, 1)
    w_2 = np.zeros((HIDP, CHUNKS, P), np.float32)
    for i in range(CHUNKS):
        first, end = CUT[i % 3], CUT[i % 3 + 1]
        w_2[0:end - first, i] = pairs[i // 3, first:end].reshape(end - first, P)
    arrays = {
        "x": c(x), "txt": c(txt), "w_tok": c(w_tok), "w_small": small, "w_exp": c(w_exp), "w_2": w_2,
        "dft": blocks.astype(np.float32), "consts": consts.astype(np.float32),
    }
    nc = bacc.Bacc("TRN2", target_bir_lowering=False, num_devices=1)
    args = {n: nc.dram_tensor(f"in_{n}", a.shape, F32, kind="ExternalInput").ap() for n, a in arrays.items()}
    out = nc.dram_tensor("out_h", [B, L, C], F32, kind="ExternalOutput").ap()
    build(nc, out=out, **args)
    r = run_bass_kernel_spmd(nc, [{f"in_{n}": a for n, a in arrays.items()}], core_ids=[0])
    return r.results[0]["out_h"]
```
